# Optimizing a Trainium2 kernel written in Bass

```python
import numpy as np
import jax
import jax.numpy as jnp

def _softmax(x, axis=-1):
    return jax.nn.softmax(x, axis=axis)

def _gelu(x):
    return jax.nn.gelu(x, approximate=True)

def _silu(x):
    return jax.nn.silu(x)

def _sigmoid(x):
    return jax.nn.sigmoid(x)

def _layernorm(x, axis=-1, eps=1e-05):
    m = jnp.mean(x, axis=axis, keepdims=True)
    v = jnp.var(x, axis=axis, keepdims=True)
    return (x - m) / jnp.sqrt(v + eps)

def _scatter_add(tgt, idx, src, axis=0):
    return tgt.at[idx].add(src)

def _segment_sum(src, seg, n):
    return jax.ops.segment_sum(src, seg, n)
kernel_name = 'mk_vit_tower_cls_d1_tok_img1024_r4_aed929'

def setup_inputs(seed: int=0):
    np.random.seed(seed)
    _w = jnp.asarray

    def _rec_inputs():
        import jax
        import jax.numpy as jnp
        _rk = jax.random.key(seed)
        x = -0.00016672 + 0.999947 * jax.random.normal(jax.random.fold_in(_rk, 1), (32, 3, 96, 96), jnp.float32)
        cls_tok = 0.02 * jax.random.normal(jax.random.fold_in(_rk, 5), (1, 1, 256), jnp.float32)
        return (x, cls_tok)
    x, cls_tok = _rec_inputs()

    def _L0_tok_setup():
        import jax, jax.numpy as jnp
        import numpy as np
        key = jax.random.key(seed)
        kx, kw, kpos = jax.random.split(key, 3)
        B, C, H, W = (64, 3, 96, 96)
        p, dim = (16, 256)
        n_patches = H // p * (W // p)
        x = jax.random.normal(kx, (B, C, H, W), dtype=jnp.float32)
        w = jax.random.normal(kw, (dim, C * p * p), dtype=jnp.float32) * 0.02
        b = jnp.zeros((dim,), dtype=jnp.float32)
        cls_token = jnp.ones((dim,), dtype=jnp.float32)
        pos = jax.random.uniform(kpos, (n_patches + 1, dim), dtype=jnp.float32)
        return {'x': x, 'w': w, 'b': b, 'cls_token': cls_token, 'pos': pos, 'patch_size': p}
    _L0_tok_all = _L0_tok_setup()
    _L0_tok_in = {k: v for k, v in _L0_tok_all.items() if k in ('w', 'b', 'cls_token', 'pos')}
    del _L0_tok_all

    def _L0_attn_setup():
        import jax, jax.numpy as jnp
        import numpy as np
        EMB = 256
        H = 16
        D = EMB // H
        EPS = 1e-05
        SM_SCALE = 1.0
        CAUSAL = True
        NEG = -1e+30

        def _layernorm(t, g, b):
            m = jnp.mean(t, axis=-1, keepdims=True)
            v = jnp.mean(jnp.square(t - m), axis=-1, keepdims=True)
            return (t - m) * jax.lax.rsqrt(v + EPS) * g + b
        key = jax.random.key(seed)
        ks = jax.random.split(key, 8)
        N, L = (2, 512)
        x = jax.random.normal(ks[0], (N, L, EMB), dtype=jnp.float32)
        mask = jnp.ones((N, L), dtype=jnp.int32)
        s = 0.02
        Wq = jax.random.normal(ks[1], (EMB, EMB), dtype=jnp.float32) * s
        Wk = jax.random.normal(ks[2], (EMB, EMB), dtype=jnp.float32) * s
        Wv = jax.random.normal(ks[3], (EMB, EMB), dtype=jnp.float32) * s
        Wo = jax.random.normal(ks[4], (EMB, EMB), dtype=jnp.float32) * s
        bo = jnp.zeros((EMB,), dtype=jnp.float32)
        gq = jnp.ones((D,), dtype=jnp.float32)
        bq = jnp.zeros((D,), dtype=jnp.float32)
        gk = jnp.ones((D,), dtype=jnp.float32)
        bk = jnp.zeros((D,), dtype=jnp.float32)
        return {'x': x, 'mask': mask, 'Wq': Wq, 'Wk': Wk, 'Wv': Wv, 'gq': gq, 'bq': bq, 'gk': gk, 'bk': bk, 'Wo': Wo, 'bo': bo}
    _L0_attn_all = _L0_attn_setup()
    _L0_attn_in = {k: v for k, v in _L0_attn_all.items() if k in ('mask', 'Wq', 'Wk', 'Wv', 'gq', 'bq', 'gk', 'bk', 'Wo', 'bo')}
    del _L0_attn_all

    def _L0_ffn_setup():
        import jax, jax.numpy as jnp
        import numpy as np
        from jax.scipy.linalg import expm
        B, S, D, E, K, NROT = (2, 512, 256, 8, 2, 3)
        EPS = 1e-05

        def _gelu(x):
            return jax.nn.gelu(x, approximate=False)

        def _forward(x, ln_gamma, ln_beta, abel_w, abel_b, moe_gate_w, moe_gate_b, ew1, eb1, ew2, eb2, gens, gc_w, gc_b):
            residual = x
            mu = jnp.mean(x, axis=-1, keepdims=True)
            var = jnp.mean((x - mu) ** 2, axis=-1, keepdims=True)
            xn = (x - mu) * jax.lax.rsqrt(var + EPS) * ln_gamma + ln_beta
            abel_out = _gelu(xn @ abel_w + abel_b)
            logits = xn @ moe_gate_w + moe_gate_b
            topw, topi = jax.lax.top_k(logits, K)
            topw = jax.nn.softmax(topw, axis=-1)
            w_dense = jnp.sum(jax.nn.one_hot(topi, E, dtype=xn.dtype) * topw[..., None], axis=-2)
            h = _gelu(jnp.einsum('bsd,edh->ebsh', xn, ew1) + eb1[:, None, None, :])
            eo = jnp.einsum('ebsh,ehd->ebsd', h, ew2) + eb2[:, None, None, :]
            moe_out = jnp.einsum('ebsd,bse->bsd', eo, w_dense)
            for i in range(NROT):
                moe_out = moe_out @ expm(gens[i])
            combined = jnp.concatenate([abel_out, moe_out], axis=-1)
            gate = jax.nn.sigmoid(combined @ gc_w + gc_b)
            mixed = abel_out * (1.0 - gate) + moe_out * gate
            return residual + mixed
        key = jax.random.key(seed)
        ks = jax.random.split(key, 16)
        sc = 0.02
        x = jax.random.normal(ks[0], (B, S, D), jnp.float32)
        ln_gamma = 1.0 + sc * jax.random.normal(ks[1], (D,), jnp.float32)
        ln_beta = sc * jax.random.normal(ks[2], (D,), jnp.float32)
        abel_w = sc * jax.random.normal(ks[3], (D, D), jnp.float32)
        abel_b = sc * jax.random.normal(ks[4], (D,), jnp.float32)
        moe_gate_w = sc * jax.random.normal(ks[5], (D, E), jnp.float32)
        moe_gate_b = sc * jax.random.normal(ks[6], (E,), jnp.float32)
        ew1 = sc * jax.random.normal(ks[7], (E, D, 2 * D), jnp.float32)
        eb1 = sc * jax.random.normal(ks[8], (E, 2 * D), jnp.float32)
        ew2 = sc * jax.random.normal(ks[9], (E, 2 * D, D), jnp.float32)
        eb2 = sc * jax.random.normal(ks[10], (E, D), jnp.float32)
        g = sc * jax.random.normal(ks[11], (NROT, D, D), jnp.float32)
        gens = 0.5 * (g - jnp.swapaxes(g, -1, -2))
        gc_w = sc * jax.random.normal(ks[12], (2 * D, 1), jnp.float32)
        gc_b = sc * jax.random.normal(ks[13], (1,), jnp.float32)
        return dict(x=x, ln_gamma=ln_gamma, ln_beta=ln_beta, abel_w=abel_w, abel_b=abel_b, moe_gate_w=moe_gate_w, moe_gate_b=moe_gate_b, ew1=ew1, eb1=eb1, ew2=ew2, eb2=eb2, gens=gens, gc_w=gc_w, gc_b=gc_b)
    _L0_ffn_all = _L0_ffn_setup()
    _L0_ffn_in = {k: v for k, v in _L0_ffn_all.items() if k in ('ln_gamma', 'ln_beta', 'abel_w', 'abel_b', 'moe_gate_w', 'moe_gate_b', 'ew1', 'eb1', 'ew2', 'eb2', 'gens', 'gc_w', 'gc_b')}
    del _L0_ffn_all
    return {'x': x, 'cls_tok': cls_tok, 'L0_tok_w': _L0_tok_in['w'], 'L0_tok_b': _L0_tok_in['b'], 'L0_tok_cls_token': _L0_tok_in['cls_token'], 'L0_tok_pos': _L0_tok_in['pos'], 'L0_attn_mask': _L0_attn_in['mask'], 'L0_attn_Wq': _L0_attn_in['Wq'], 'L0_attn_Wk': _L0_attn_in['Wk'], 'L0_attn_Wv': _L0_attn_in['Wv'], 'L0_attn_gq': _L0_attn_in['gq'], 'L0_attn_bq': _L0_attn_in['bq'], 'L0_attn_gk': _L0_attn_in['gk'], 'L0_attn_bk': _L0_attn_in['bk'], 'L0_attn_Wo': _L0_attn_in['Wo'], 'L0_attn_bo': _L0_attn_in['bo'], 'L0_ffn_ln_gamma': _L0_ffn_in['ln_gamma'], 'L0_ffn_ln_beta': _L0_ffn_in['ln_beta'], 'L0_ffn_abel_w': _L0_ffn_in['abel_w'], 'L0_ffn_abel_b': _L0_ffn_in['abel_b'], 'L0_ffn_moe_gate_w': _L0_ffn_in['moe_gate_w'], 'L0_ffn_moe_gate_b': _L0_ffn_in['moe_gate_b'], 'L0_ffn_ew1': _L0_ffn_in['ew1'], 'L0_ffn_eb1': _L0_ffn_in['eb1'], 'L0_ffn_ew2': _L0_ffn_in['ew2'], 'L0_ffn_eb2': _L0_ffn_in['eb2'], 'L0_ffn_gens': _L0_ffn_in['gens'], 'L0_ffn_gc_w': _L0_ffn_in['gc_w'], 'L0_ffn_gc_b': _L0_ffn_in['gc_b']}

def reference(x, cls_tok, L0_tok_w, L0_tok_b, L0_tok_cls_token, L0_tok_pos, L0_attn_mask, L0_attn_Wq, L0_attn_Wk, L0_attn_Wv, L0_attn_gq, L0_attn_bq, L0_attn_gk, L0_attn_bk, L0_attn_Wo, L0_attn_bo, L0_ffn_ln_gamma, L0_ffn_ln_beta, L0_ffn_abel_w, L0_ffn_abel_b, L0_ffn_moe_gate_w, L0_ffn_moe_gate_b, L0_ffn_ew1, L0_ffn_eb1, L0_ffn_ew2, L0_ffn_eb2, L0_ffn_gens, L0_ffn_gc_w, L0_ffn_gc_b):
    import jax
    import jax.numpy as jnp

    def _L0_tok_ref(x, w, b, cls_token, pos, patch_size):
        import jax, jax.numpy as jnp
        import numpy as np
        B, C, H, W = x.shape
        p = patch_size
        Hp, Wp = (H // p, W // p)
        dim = w.shape[0]
        patches = x.reshape(B, C, Hp, p, Wp, p).transpose(0, 2, 4, 1, 3, 5).reshape(B, Hp * Wp, C * p * p)
        tokens = jnp.einsum('bnf,df->bnd', patches, w) + b
        cls = jnp.broadcast_to(cls_token, (B, 1, dim))
        emb = jnp.concatenate([cls, tokens], axis=1)
        return emb + pos

    def _L0_attn_ref(x, mask, Wq, Wk, Wv, gq, bq, gk, bk, Wo, bo):
        import jax, jax.numpy as jnp
        import numpy as np
        EMB = 256
        H = 16
        D = EMB // H
        EPS = 1e-05
        SM_SCALE = 1.0
        CAUSAL = True
        NEG = -1e+30

        def _layernorm(t, g, b):
            m = jnp.mean(t, axis=-1, keepdims=True)
            v = jnp.mean(jnp.square(t - m), axis=-1, keepdims=True)
            return (t - m) * jax.lax.rsqrt(v + EPS) * g + b
        N, L, _ = x.shape
        q = (x @ Wq.T).reshape(N, L, H, D).transpose(0, 2, 1, 3)
        k = (x @ Wk.T).reshape(N, L, H, D).transpose(0, 2, 1, 3)
        v = (x @ Wv.T).reshape(N, L, H, D).transpose(0, 2, 1, 3)
        q = _layernorm(q, gq, bq)
        k = _layernorm(k, gk, bk)
        scores = jnp.einsum('nhld,nhmd->nhlm', q, k) * SM_SCALE
        if CAUSAL:
            causal = jnp.tril(jnp.ones((L, L), dtype=bool))
            scores = jnp.where(causal, scores, NEG)
        attn = jax.nn.softmax(scores, axis=-1)
        out = jnp.einsum('nhlm,nhmd->nhld', attn, v)
        out = out.transpose(0, 2, 1, 3).reshape(N, L, EMB)
        return out @ Wo.T + bo

    def _L0_ffn_ref(x, ln_gamma, ln_beta, abel_w, abel_b, moe_gate_w, moe_gate_b, ew1, eb1, ew2, eb2, gens, gc_w, gc_b):
        import jax, jax.numpy as jnp
        import numpy as np
        from jax.scipy.linalg import expm
        B, S, D, E, K, NROT = (2, 512, 256, 8, 2, 3)
        EPS = 1e-05

        def _gelu(x):
            return jax.nn.gelu(x, approximate=False)

        def _forward(x, ln_gamma, ln_beta, abel_w, abel_b, moe_gate_w, moe_gate_b, ew1, eb1, ew2, eb2, gens, gc_w, gc_b):
            residual = x
            mu = jnp.mean(x, axis=-1, keepdims=True)
            var = jnp.mean((x - mu) ** 2, axis=-1, keepdims=True)
            xn = (x - mu) * jax.lax.rsqrt(var + EPS) * ln_gamma + ln_beta
            abel_out = _gelu(xn @ abel_w + abel_b)
            logits = xn @ moe_gate_w + moe_gate_b
            topw, topi = jax.lax.top_k(logits, K)
            topw = jax.nn.softmax(topw, axis=-1)
            w_dense = jnp.sum(jax.nn.one_hot(topi, E, dtype=xn.dtype) * topw[..., None], axis=-2)
            h = _gelu(jnp.einsum('bsd,edh->ebsh', xn, ew1) + eb1[:, None, None, :])
            eo = jnp.einsum('ebsh,ehd->ebsd', h, ew2) + eb2[:, None, None, :]
            moe_out = jnp.einsum('ebsd,bse->bsd', eo, w_dense)
            for i in range(NROT):
                moe_out = moe_out @ expm(gens[i])
            combined = jnp.concatenate([abel_out, moe_out], axis=-1)
            gate = jax.nn.sigmoid(combined @ gc_w + gc_b)
            mixed = abel_out * (1.0 - gate) + moe_out * gate
            return residual + mixed
        return _forward(x, ln_gamma, ln_beta, abel_w, abel_b, moe_gate_w, moe_gate_b, ew1, eb1, ew2, eb2, gens, gc_w, gc_b)
    h = _L0_tok_ref(x, L0_tok_w, L0_tok_b, L0_tok_cls_token, L0_tok_pos, 16)
    h = jnp.concatenate([jnp.broadcast_to(cls_tok, (h.shape[0], 1, h.shape[2])), h], axis=1)
    h = h + _L0_attn_ref(_layernorm(h, axis=-1), L0_attn_mask, L0_attn_Wq, L0_attn_Wk, L0_attn_Wv, L0_attn_gq, L0_attn_bq, L0_attn_gk, L0_attn_bk, L0_attn_Wo, L0_attn_bo)
    h = h + _L0_ffn_ref(_layernorm(h, axis=-1), L0_ffn_ln_gamma, L0_ffn_ln_beta, L0_ffn_abel_w, L0_ffn_abel_b, L0_ffn_moe_gate_w, L0_ffn_moe_gate_b, L0_ffn_ew1, L0_ffn_eb1, L0_ffn_ew2, L0_ffn_eb2, L0_ffn_gens, L0_ffn_gc_w, L0_ffn_gc_b)
    return h

_drawn_inputs = setup_inputs


def setup_inputs(seed=0):
    import zlib

    import numpy as np

    out = dict(_drawn_inputs(seed))
    spreads = {'L0_tok_b': (0.0, 0.1),
     'L0_tok_cls_token': (1.0, 0.2),
     'L0_attn_gq': (1.0, 0.2),
     'L0_attn_bq': (0.0, 0.715),
     'L0_attn_gk': (1.0, 0.2),
     'L0_attn_bk': (0.0, 2.0),
     'L0_attn_bo': (0.0, 0.1)}
    factors = {'L0_ffn_ln_gamma': 8.0,
     'L0_ffn_ln_beta': 8.0,
     'L0_ffn_abel_b': 24.575,
     'L0_ffn_moe_gate_w': 3.786,
     'L0_ffn_moe_gate_b': 8.0,
     'L0_ffn_ew1': 3.546,
     'L0_ffn_eb1': 8.0,
     'L0_ffn_ew2': 3.456,
     'L0_ffn_eb2': 22.814,
     'L0_ffn_gens': 8.0,
     'L0_ffn_gc_w': 8.0}
    for name, (base, spread) in spreads.items():
        noise = np.random.default_rng([zlib.crc32(name.encode()), seed]).standard_normal(out[name].shape)
        drawn = base * np.exp(spread * noise) if base else spread * noise
        out[name] = jnp.asarray(drawn.astype(out[name].dtype))
    for name, factor in factors.items():
        out[name] = (out[name] * factor).astype(out[name].dtype)
    return out
```

```python
from contextlib import ExitStack

import concourse.bass as bass
import numpy as np
from concourse import mybir

B, SEQ, D = 32, 38, 256
IPT = 3
T = IPT * SEQ
NT = -(-B // IPT)
TLAST = B * SEQ - (NT - 1) * T
FK = 6
NH, HD = 16, 16
VW = HD + 1
E, HID = 8, 512
NS = (2 * B * SEQ + E * 127) // 128
PW = D + E
EPS = 1e-5
NEG = -1e30
G = 3
SQUARINGS = 4
THETA = 1.7
EXPM_LIMIT = 3.925724783138660 * 2.0 ** 17

C_GQ, C_BQ, C_GK, C_BK, C_GAM, C_BET, C_EPS = 0, 1, 2, 4, 6, 8, 10
NCOL = 12
R_BASE, R_POS, R_BO, R_PRE, R_GW, R_GCB = 0, D, 2 * D, 3 * D, 3 * D + PW, 5 * D + PW
NROW = 5 * D + PW + 1
K_ID, K_MASK, K_LOW, K_ONE, K_IOTA, K_INV, K_SEG, K_SEG8 = 0, 128, 256, 384, 512, 544, 566, 654
NCONST = 664


def vit_kernel(nc, patches, w_tok, w_qkv, w_o, w_pre, w1, w2, b1, b2, gens, gens_t,
               cols, rows, consts, out):
    fp32, bf16, i32, u32 = mybir.dt.float32, mybir.dt.bfloat16, mybir.dt.int32, mybir.dt.uint32
    ALU, ACT, AX = mybir.AluOpType, mybir.ActivationFunctionType, mybir.AxisListType
    ds = bass.ds
    ctx = ExitStack()
    with ctx:
        def sb(name, width, dt=fp32):
            return ctx.enter_context(nc.sbuf_tensor(name, [128, width], dt))

        def sem(name):
            return ctx.enter_context(nc.semaphore(name))

        xs_dram = nc.dram_tensor("xs_rows", (NS * 128, D), fp32, kind="Internal").ap()
        ys_dram = nc.dram_tensor("ys_rows", (NS * 128, D), fp32, kind="Internal").ap()

        patch_sb = sb("patch_sb", 4 * FK * T)
        wtok_sb = sb("wtok_sb", FK * D)
        wqkv_sb = sb("wqkv_sb", 2 * 3 * D)
        wo_sb = sb("wo_sb", 2 * D)
        wpre_sb = sb("wpre_sb", 2 * PW)
        w1_sb = sb("w1_sb", E * 2 * HID)
        w2_sb = sb("w2_sb", E * 4 * D)
        col_sb = sb("col_sb", NCOL)
        row_sb = sb("row_sb", NROW)
        con_sb = sb("con_sb", NCONST)
        idb_sb = sb("idb_sb", T, bf16)
        maskb_sb = sb("maskb_sb", T, bf16)
        h_sb = sb("h_sb", NT * D)
        hb_sb = sb("hb_sb", NT * D)
        h1_sb = sb("h1_sb", NT * D)
        qk_sb = sb("qk_sb", NT * 2 * D)
        v_sb = sb("v_sb", NT * NH * VW)
        stage_sb = sb("stage_sb", 2 * D)
        xT_sb = sb("xT_sb", 2 * 2 * T)
        sq_sb = sb("sq_sb", 2 * 2 * D)
        qn_sb = sb("qn_sb", 2 * 2 * D)
        qkT_sb = sb("qkT_sb", 2 * 6 * T)
        p_sb = sb("p_sb", 2 * NH * T)
        pT_sb = sb("pT_sb", 2 * 4 * T)
        att_sb = sb("att_sb", 2 * D)
        attT_sb = sb("attT_sb", 2 * T)
        mv_sb = sb("mv_sb", 2 * NT)
        mv2_sb = sb("mv2_sb", 2 * NT)
        ss_sb = sb("ss_sb", NT * 2 * NH)
        half_sb = sb("half_sb", 1)
        r1_sb = sb("r1_sb", NT)
        rr_sb = sb("rr_sb", 6 * NT)
        mx_sb = sb("mx_sb", NH)
        rc_sb = sb("rc_sb", NH)
        idx_sb = sb("idx_sb", NT * 8, u32)
        rti_sb = sb("rti_sb", E, i32)
        ei_sb = sb("ei_sb", NS, i32)
        slot_sb = sb("slot_sb", 2 * NT, i32)
        wt_sb = sb("wt_sb", 4 * NT)
        z_sb = sb("z_sb", 4 * NT)
        nrm_sb = sb("nrm_sb", 16)
        nrmi_sb = sb("nrmi_sb", 4, i32)

        def tri(t_, k, w):
            return t_[0:T, ds(k * w, w)]

        b2_sb = p_sb[:, 0:E * D]
        y_sb = p_sb[:, E * D:E * D + G * 512]
        yT_sb = wtok_sb
        b1_sb = qk_sb[:, 0:E * HID]
        a_sb, aT_sb = patch_sb[:, 0:G * 512], wqkv_sb
        keep_v_sb = sq_sb[:, 0:2 * NH * VW]
        newton_sb = p_sb[:, 0:2 * NT * 2 * NH]
        A2 = [qk_sb[:, n * 512:(n + 1) * 512] for n in range(G)]
        A3 = [qk_sb[:, (3 + n) * 512:(4 + n) * 512] for n in range(G)]
        A4 = [qk_sb[:, (6 + n) * 512:(7 + n) * 512] for n in range(G)]
        poly = [qk_sb[:, 9 * 512:10 * 512], qk_sb[:, 10 * 512:11 * 512], qkT_sb[:, 0:512]]
        A4T = [qkT_sb[:, 512:1024], sq_sb[:, 0:512], sq_sb[:, 512:1024]]
        A = [a_sb[:, n * 512:(n + 1) * 512] for n in range(G)]
        AT = [aT_sb[:, n * 512:(n + 1) * 512] for n in range(G)]
        Y = [y_sb[:, n * 512:(n + 1) * 512] for n in range(G)]
        YT = [yT_sb[:, n * 512:(n + 1) * 512] for n in range(G)]
        hid_sb, hidT_sb = sq_sb, stage_sb
        zero_sb = h1_sb[:, 0:NS * D // 4]
        rt_sb = sq_sb[:, 0:8 * E * NT]
        cmp_sb = pT_sb[:, 0:NS * E]
        wc_sb = pT_sb[:, 256:256 + 4 * NH]
        rt8_sb = pT_sb[:, 320:320 + 8 * E]
        ef_sb = pT_sb[:, 384:384 + NS]
        top_sb = att_sb[:, 0:NT * 8]
        stat_sb = idx_sb[:, 0:NT * 6].bitcast(fp32)
        xs_sb, xsT_sb = qn_sb[:, 0:2 * D], qn_sb[:, 2 * D:4 * D]
        ys_sb = pT_sb

        bank = [ctx.enter_context(nc.psum_tensor(f"bank{n}", [128, 512], fp32)) for n in range(8)]

        d_tok = [sem(f"d_tok{k}") for k in range(FK)]
        d_con, d_qkv, d_w, d_exp = sem("d_con"), sem("d_qkv"), sem("d_w"), sem("d_exp")
        d_patch = [sem(f"d_patch{n}") for n in range(4)]
        d_zero, d_b, d_gen, d_scat = sem("d_zero"), sem("d_b"), sem("d_gen"), sem("d_scat")
        d_xs = [sem("d_xs0"), sem("d_xs1")]
        d_ys_c1 = [sem("d_ys0_c1"), sem("d_ys1_c1")]
        d_gather = [sem(f"d_gather{n}") for n in range(NT)]
        d_out = sem("d_out")
        consts_set, zero_set, half_set = sem("consts_set"), sem("zero_set"), sem("half_set")
        dve_chain, pool_chain = sem("dve_chain"), sem("pool_chain")
        embedded, h_added_cr = sem("embedded"), sem("h_added_cr")
        stats1, rstd1, hb_set = sem("stats1"), sem("rstd1"), sem("hb_set")
        w_centred, xh_set, xh_turned, xT_set_cr = sem("w_centred"), sem("xh_set"), sem("xh_turned"), sem("xT_set_cr")
        qk_made, v_made, qk_squared_cr, v_kept_cr, ss_set_cr = (
            sem("qk_made"), sem("v_made"), sem("qk_squared_cr"), sem("v_kept_cr"), sem("ss_set_cr"))
        rstd_qk = sem("rstd_qk")
        qn_set, turned, evac_cr = sem("qn_set"), sem("turned"), sem("evac_cr")
        scored, shifted_cr, max_set, probs_set = sem("scored"), sem("shifted_cr"), sem("max_set"), sem("probs_set")
        pv_made, rc_set, att_set_c1, wo_made, h1_added_c1 = (
            sem("pv_made"), sem("rc_set"), sem("att_set"), sem("wo_made"), sem("h1_added"))
        h1_stats, rstd2 = sem("h1_stats"), sem("rstd2")
        zs_set, z_turned, zT_set_cr, pre_made, pre_kept_cr = (
            sem("zs_set"), sem("z_turned"), sem("zT_set_cr"), sem("pre_made"), sem("pre_kept_cr"))
        top_set, idx_set, abel_set = sem("top_set"), sem("idx_set"), sem("abel_set")
        onehot_set, ranked, slots_set, experts_set = sem("onehot_set"), sem("ranked"), sem("slots_set"), sem("experts_set")
        gap_set, ratio_set, resid_set, abelw_set = sem("gap_set"), sem("ratio_set"), sem("resid_set"), sem("abelw_set")
        n_part, n_max, n_scaled, v_staged = sem("n_part"), sem("n_max"), sem("n_scaled"), sem("v_staged")
        x_made, x_kept, x_turned, x_evac, p_made, y_set = (
            sem("x_made"), sem("x_kept"), sem("x_turned"), sem("x_evac"), sem("p_made"), sem("y_set"))
        var_set, root_set = sem("var_set"), sem("root_set")
        z_bounded = sem("z_bounded")
        poly_set, stats_done = sem("poly_set"), sem("stats_done")
        s_made, s_kept_cr, s_turned, s_evac = sem("s_made"), sem("s_kept_cr"), sem("s_turned"), sem("s_evac")
        e_made, e_kept, e_turned, e_evac = sem("e_made"), sem("e_kept"), sem("e_turned"), sem("e_evac")
        xs_turned, xsT_set, hid_made, hid_biased_cr, gelu_set = (
            sem("xs_turned"), sem("xsT_set"), sem("hid_made"), sem("hid_biased_cr"), sem("gelu_set"))
        hid_turned_c1, hidT_set_c1, ys_made, ys_set_cr = sem("hid_turned_c1"), sem("hidT_set_c1"), sem("ys_made"), sem("ys_set_cr")
        m1_set, moe_set, moe_turned, moeT_set, rot_made, rot_kept, z_set = (
            sem("m1_set"), sem("moe_set"), sem("moe_turned"), sem("moeT_set"), sem("rot_made"), sem("rot_kept"), sem("z_set"))
        gexp_set, gate_set, diff_set, out_set = sem("gexp_set"), sem("gate_set"), sem("diff_set"), sem("out_set")

        ident = con_sb[:, K_ID:K_ID + 128]
        identT = con_sb[0:T, K_ID:K_ID + T]

        def col(c):
            return col_sb[:, c:c + 1]

        def pairs(eng, step, n):
            with eng.Fori(0, n // 2) as i:
                step(2 * i, 0)
                step(2 * i + 1, 1)

        def uses(t):
            known = isinstance(t, int)
            names = ["T"] * (not known or t <= NT - 3) + ["P0", "P1"] + ["A"] * (not known or t > 0) + ["P2", "P3"]
            if known:
                first = 2 + sum(len(uses(n)) for n in range(t)) if t else 2
            else:
                first = 6 * t + 1
            return {name: (first + n, (first + n) % 2 if known else (1 + n) % 2) for n, name in enumerate(names)}

        LAST_USE = (6 * NT - 1, 1)

        def real(t):
            return T if t < NT - 1 else TLAST

        def last_tile(t):
            return isinstance(t, int) and t == NT - 1

        def attn_tiles(eng, step):
            step(0, 0)
            step(1, 1)
            with eng.Fori(1, 4) as i:
                step(2 * i, 0)
                step(2 * i + 1, 1)
            for t in range(8, NT):
                step(t, t % 2)

        block = ctx.enter_context(nc.Block())

        @block.sync
        def _(sp):
            sp.sem_inc(d_ys_c1[0], 16)
            sp.sem_inc(d_ys_c1[1], 16)
            sp.dma_start(patch_sb[:, 0:FK * T], patches[0]).then_inc(d_patch[0], 16)
            for k in range(FK):
                sp.dma_start(wtok_sb[:, k * D:(k + 1) * D], w_tok[:, k * D:(k + 1) * D]).then_inc(d_tok[k], 16)
            for t in range(1, 4):
                sp.dma_start(patch_sb[:, t * FK * T:(t + 1) * FK * T], patches[t]).then_inc(d_patch[t], 16)
            sp.dma_start(con_sb[:, :], consts).then_inc(d_con, 16)
            sp.dma_start(wqkv_sb[:, :], w_qkv).then_inc(d_qkv, 16)
            for t in range(4, NT):
                sp.wait_ge(embedded, t - 3)
                s = t % 4
                sp.dma_start(patch_sb[:, s * FK * T:(s + 1) * FK * T], patches[t]).then_inc(d_patch[s], 16)
            sp.dma_start(wo_sb[:, :], w_o).then_inc(d_w, 16)
            sp.dma_start(wpre_sb[:, :], w_pre).then_inc(d_w, 16)
            sp.wait_ge(zero_set, 1)
            zview = xs_dram.rearrange("(p a) d -> p (a d)", p=128)
            ZW = NS * D // 4
            for n in range(4):
                sp.dma_start(zview[:, n * ZW:(n + 1) * ZW], zero_sb).then_inc(d_zero, 16)
            sp.dma_start(w1_sb[:, :], w1).then_inc(d_exp, 16)
            sp.dma_start(w2_sb[:, :], w2).then_inc(d_exp, 16)
            sp.wait_ge(embedded, NT)
            sp.dma_start(a_sb, gens).then_inc(d_gen, 16)
            sp.wait_ge(v_made, NT)
            sp.dma_start(aT_sb[:, :], gens_t).then_inc(d_gen, 16)
            sp.wait_ge(h1_added_c1, NT + 1)
            sp.dma_start(b2_sb, b2.broadcast_to([128, E * D])).then_inc(d_b, 16)

            def load(j, s):
                sp.dma_start(xs_sb[:, s * D:(s + 1) * D], xs_dram[ds(j * 128, 128), :]).then_inc(d_xs[s], 16)

            def store(j, s):
                sp.wait_ge(ys_set_cr, j + 3)
                sp.dma_start(ys_dram[ds(j * 128, 128), :], ys_sb[:, s * D:(s + 1) * D]).then_inc(d_ys_c1[s], 16)

            def slot_step(j, s):
                sp.wait_ge(xs_turned, j + 3)
                load(j + 4, s)
                store(j, s)

            sp.wait_ge(d_scat, 16 * 2 * NT)
            load(0, 0)
            load(1, 1)
            sp.wait_ge(y_set, G)
            sp.dma_start(b1_sb, b1.broadcast_to([128, E * HID])).then_inc(d_b, 16)
            for j in range(2):
                sp.wait_ge(xs_turned, j + 1)
                load(j + 2, j)
            pairs(sp, slot_step, NS - 4)
            for j in range(NS - 4, NS):
                store(j, j % 2)

            def out_tile(t):
                sp.wait_ge(out_set, t + 1)
                sp.dma_start(out[ds(t * T, T), :], h1_sb[0:T, ds(t * D, D)]).then_inc(d_out, 16)

            with sp.Fori(0, NT - 1) as t:
                out_tile(t)
            sp.wait_ge(out_set, NT)
            sp.dma_start(out[(NT - 1) * T:B * SEQ, :], h1_sb[0:TLAST, (NT - 1) * D:NT * D]).then_inc(d_out, 16)
            sp.wait_ge(d_out, 16 * NT)

        @block.gpsimd
        def _(pool):
            count = [0]

            def link(ins):
                count[0] += 1
                ins.then_inc(pool_chain, 1)
                pool.wait_ge(pool_chain, count[0])

            pool.memset(zero_sb, 0.0).then_inc(zero_set, 1)
            pool.memset(half_sb[:, :], -0.5).then_inc(half_set, 1)
            pool.memset(v_sb[:, :], 1.0).then_inc(half_set, 1)
            pool.wait_ge(half_set, 2)

            def rstd_of(a, b, count):
                pool.wait_ge(stats1, count)
                var1 = mv_sb[0:T, 2 * a:2 * b].rearrange("p (t c) -> p t c", c=2)[:, :, 1]
                link(pool.tensor_scalar(r1_sb[0:T, a:b], var1, EPS, None, ALU.add))
                pool.tensor_tensor(r1_sb[0:T, a:b], r1_sb[0:T, a:b], half_sb[0:T, :].broadcast_to([T, b - a]),
                                   ALU.pow).then_inc(rstd1, 1)

            rstd_of(0, 8, 8)
            rstd_of(8, NT, NT)
            bo = row_sb[0:T, R_BO:R_BO + D].unsqueeze(1).broadcast_to([T, NT, D])
            pool.tensor_tensor(hb_sb[0:T, :].rearrange("p (t d) -> p t d", d=D),
                               h_sb[0:T, :].rearrange("p (t d) -> p t d", d=D), bo, ALU.add).then_inc(hb_set, 1)

            def stage_v(t, s):
                pool.tensor_copy(keep_v_sb[0:T, s * NH * VW:(s + 1) * NH * VW], v_sb[0:T, ds(t * NH * VW, NH * VW)]).then_inc(v_staged, 1)

            def stage_step(t, s):
                pool.wait_ge(pv_made, 4 * t + 4)
                stage_v(t + 2, s)

            pool.wait_ge(ss_set_cr, NT + 2)
            stage_v(0, 0)
            stage_v(1, 1)
            pairs(pool, stage_step, 8)
            pool.wait_ge(n_part, 1)
            pool.partition_all_reduce(nrm_sb[:, 7:8], nrm_sb[:, 6:7], 128, bass.bass_isa.ReduceOp.max).then_inc(n_max, 1)
            stage_step(NT - 3, 0)

            def rstd_pair(a, b, count):
                pool.wait_ge(h1_stats, count)
                v2 = mv2_sb[0:T, 2 * a:2 * b].rearrange("p (t c) -> p t c", c=2)[:, :, 1]
                m2 = mv2_sb[0:T, 2 * a:2 * b].rearrange("p (t c) -> p t c", c=2)[:, :, 0]
                half = half_sb[0:T, :].broadcast_to([T, b - a])
                R = [rr_sb[0:T, n * NT + a:n * NT + b] for n in range(5)]
                link(pool.tensor_scalar(R[0], v2, EPS, None, ALU.add))
                link(pool.tensor_scalar(R[1], R[0], EPS, None, ALU.mult))
                link(pool.tensor_tensor(R[1], R[1], v2, ALU.add))
                link(pool.tensor_tensor(R[0], R[0], half, ALU.pow))
                link(pool.tensor_tensor(R[1], R[1], half, ALU.pow))
                link(pool.tensor_tensor(R[2], m2, R[1], ALU.mult))
                link(pool.tensor_scalar(R[2], R[2], -1.0, None, ALU.mult))
                link(pool.tensor_tensor(R[3], m2, R[0], ALU.mult))
                link(pool.tensor_scalar(R[3], R[3], -1.0, None, ALU.mult))
                pool.tensor_scalar(R[4], R[0], 1.0, None, ALU.add).then_inc(rstd2, 1)

            rstd_pair(0, 8, 8)
            rstd_pair(8, NT, NT)
            pool.wait_ge(d_zero, 16 * 4)
            pool.wait_ge(slots_set, 2)
            for t in range(NT):
                n = T if t < NT - 1 else TLAST
                for c in range(2):
                    pool.indirect_dma_start(
                        out=xs_dram, out_offset=bass.IndirectOffsetOnAxis(ap=slot_sb[0:n, c * NT + t:c * NT + t + 1].bitcast(u32), axis=0),
                        in_=h_sb[0:n, t * D:(t + 1) * D], in_offset=None).then_inc(d_scat, 16)
            pool.wait_ge(abel_set, 1)
            pool.wait_ge(resid_set, 1)
            ab3 = h1_sb[0:T, :].rearrange("p (t d) -> p t d", d=D)
            hb3 = hb_sb[0:T, :].rearrange("p (t d) -> p t d", d=D)
            pool.tensor_tensor(hb3, hb3, ab3, ALU.add).then_inc(abelw_set, 1)
            pool.wait_ge(d_ys_c1[0], 16 * (NS // 2 + 1))
            pool.wait_ge(d_ys_c1[1], 16 * (NS // 2 + 1))
            for t in range(NT):
                n = T if t < NT - 1 else TLAST
                for c in range(2):
                    pool.indirect_dma_start(
                        out=qk_sb[0:n, (c * NT + t) * D:(c * NT + t + 1) * D], out_offset=None, in_=ys_dram,
                        in_offset=bass.IndirectOffsetOnAxis(ap=slot_sb[0:n, c * NT + t:c * NT + t + 1].bitcast(u32), axis=0)).then_inc(d_gather[t], 16)

        @block.scalar
        def _(act):
            act.dma_start(row_sb[:, :], rows).then_inc(d_con, 16)
            act.dma_start(col_sb[:, :], cols).then_inc(d_con, 16)
            act.sem_inc(xT_set_cr, 2)
            act.sem_inc(qk_squared_cr, 2)
            act.sem_inc(evac_cr, 2)
            act.sem_inc(zT_set_cr, 2)
            act.sem_inc(hidT_set_c1, 1)

            def keep_xT(t, s):
                act.wait_ge(xh_turned, t + 1)
                nc.scalar.activation(xT_sb[:, s * 2 * T:(s + 1) * 2 * T], bank[s][:, 0:2 * T], ACT.Copy).then_inc(xT_set_cr, 1)

            def qkv_step(t, s, more=True):
                if more:
                    keep_xT(t + 1, 1 - s)
                act.wait_ge(qk_made, t + 1)
                nc.scalar.activation(qk_sb[0:T, ds(t * 2 * D, 2 * D)], bank[4 + s][0:T, :], ACT.Copy)
                act.wait_ge(ss_set_cr, t + 1)
                nc.scalar.activation(sq_sb[0:T, s * 2 * D:(s + 1) * 2 * D], bank[4 + s][0:T, :], ACT.Square).then_inc(qk_squared_cr, 1)

            act.wait_ge(d_con, 48)
            keep_xT(0, 0)
            def root(n):
                a, b = (0, 8 * 2 * NH) if n == 0 else (8 * 2 * NH, NT * 2 * NH)
                act.wait_ge(var_set, n + 1)
                nc.scalar.activation(newton_sb[0:T, a:b], ss_sb[0:T, a:b], ACT.Sqrt).then_inc(root_set, 1)

            pairs(act, qkv_step, 8)
            root(0)
            qkv_step(NT - 3, 0)
            qkv_step(NT - 2, 1)
            qkv_step(NT - 1, 0, False)
            root(1)

            def keep_qkT(u, s, b):
                act.wait_ge(turned, u + 1)
                qT = qkT_sb[:, s * 6 * T:s * 6 * T + 2 * T]
                kT = qkT_sb[:, s * 6 * T + 2 * T:(s + 1) * 6 * T].rearrange("p (c j m) -> p c j m", c=2, j=2)
                nc.scalar.activation(qT, bank[b][:, 0:2 * T], ACT.Identity, scale=col(C_GQ), bias=col(C_BQ))
                for j in range(2):
                    last = nc.scalar.activation(kT[:, :, j, :], bank[b][:, 2 * T:4 * T].rearrange("p (c m) -> p c m", c=2),
                                                ACT.Identity, scale=col(C_GK + j), bias=col(C_BK + j))
                last.then_inc(evac_cr, 1)

            def exp_half(t, s, hf):
                act.wait_ge(shifted_cr, 2 * t + hf + 3)
                p = p_sb[0:T, (s * NH + hf * 8) * T:(s * NH + hf * 8 + 8) * T]
                nc.scalar.activation(p, p, ACT.Exp).then_inc(probs_set, 1)

            def keep_pT(u, b, g):
                act.wait_ge(turned, u + 1)
                nc.scalar.activation(pT_sb[0:T, (g % 2) * 4 * T:(g % 2 + 1) * 4 * T], bank[b][0:T, 0:4 * T], ACT.Copy).then_inc(evac_cr, 1)

            def keep_attT(u, b):
                act.wait_ge(turned, u + 1)
                nc.scalar.activation(attT_sb[:, :], bank[b][:, 0:2 * T], ACT.Copy).then_inc(evac_cr, 1)

            def attn_step(t, s):
                u = uses(t)
                if "T" in u:
                    keep_qkT(*u["T"][0:1], s, u["T"][1])
                keep_pT(*u["P0"], 0)
                keep_pT(*u["P1"], 1)
                if "A" in u:
                    keep_attT(*u["A"])
                keep_pT(*u["P2"], 2)
                keep_pT(*u["P3"], 3)
                if not last_tile(t):
                    exp_half(t + 1, 1 - s, 0)
                    exp_half(t + 1, 1 - s, 1)

            keep_qkT(0, 0, 0)
            keep_qkT(1, 1, 1)
            exp_half(0, 0, 0)
            exp_half(0, 0, 1)
            attn_tiles(act, attn_step)
            keep_attT(*LAST_USE)

            act.wait_ge(rstd2, 1)

            def stage_z(t, s):
                nc.scalar.activation(stage_sb[0:T, s * D:(s + 1) * D], h1_sb[0:T, ds(t * D, D)], ACT.Identity,
                                     scale=rr_sb[0:T, ds(NT + t, 1)], bias=rr_sb[0:T, ds(2 * NT + t, 1)]).then_inc(zs_set, 1)

            def keep_zT(t, s):
                act.wait_ge(z_turned, t + 1)
                for c in range(2):
                    last = nc.scalar.activation(xT_sb[:, (2 * s + c) * T:(2 * s + c + 1) * T], bank[s][:, c * T:(c + 1) * T],
                                                ACT.Identity, scale=col(C_GAM + c), bias=col(C_BET + c))
                last.then_inc(zT_set_cr, 1)

            def pre_step(t, s, ahead=2):
                if ahead == 2:
                    act.wait_ge(z_turned, t + 1)
                    stage_z(t + 2, s)
                if ahead >= 1:
                    keep_zT(t + 1, 1 - s)

            stage_z(0, 0)
            stage_z(1, 1)
            keep_zT(0, 0)
            act.wait_ge(rstd2, 2)
            pairs(act, pre_step, NT - 3)
            pre_step(NT - 3, 0)
            pre_step(NT - 2, 1, 1)
            act.wait_ge(gap_set, 1)
            nc.scalar.activation(wt_sb[0:T, NT:2 * NT], wt_sb[0:T, 0:NT], ACT.Exp).then_inc(ratio_set, 1)
            act.wait_ge(pre_kept_cr, NT + 2)
            nc.scalar.activation(h1_sb[0:T, :].rearrange("p (t d) -> p t d", d=D),
                                 v_sb[0:T, 0:NT * PW].rearrange("p (t d) -> p t d", d=PW)[:, :, 0:D], ACT.Gelu).then_inc(abel_set, 1)
            x = 0
            for dst, b0 in ((A2, 5), (A3, 2), (A4, 5)):
                for n in range(G):
                    x += 1
                    act.wait_ge(x_made, x)
                    nc.scalar.activation(dst[n], bank[b0 + n][:, :], ACT.Copy).then_inc(x_kept, 1)
            act.wait_ge(slots_set, 2)
            for n in range(G):
                act.wait_ge(x_turned, n + 1)
                nc.scalar.activation(A4T[n], bank[n % 2][:, :], ACT.Copy).then_inc(x_evac, 1)
            squarings = act.value_load(nrmi_sb[0:1, 2:3], min_val=SQUARINGS, max_val=20)
            with act.Fori(0, squarings) as j:
                for n in range(G):
                    act.wait_ge(s_turned, 3 * j + n + 1)
                    nc.scalar.activation(YT[n], bank[n][:, :], ACT.Copy).then_inc(s_evac, 1)

            def keep_xsT(j, s):
                act.wait_ge(xs_turned, j + 1)
                for c in range(2):
                    last = nc.scalar.activation(xsT_sb[:, (2 * s + c) * 128:(2 * s + c + 1) * 128], bank[1][:, c * 128:(c + 1) * 128],
                                                ACT.Identity, scale=col(C_GAM + c), bias=col(C_BET + c))
                last.then_inc(xsT_set, 1)

            def gelu(j, s):
                act.wait_ge(hid_biased_cr, j + 3)
                hid = hid_sb[:, s * HID:(s + 1) * HID]
                nc.scalar.activation(hid, hid, ACT.Gelu).then_inc(gelu_set, 1)

            def slot_step(j, s, ahead=2):
                act.wait_ge(hid_turned_c1, j + 2)
                nc.scalar.activation(hidT_sb[:, :], bank[0][:, :], ACT.Copy).then_inc(hidT_set_c1, 1)
                if ahead == 2:
                    keep_xsT(j + 2, s)
                if ahead >= 1:
                    gelu(j + 1, 1 - s)

            keep_xsT(0, 0)
            keep_xsT(1, 1)
            gelu(0, 0)
            pairs(act, slot_step, NS - 2)
            slot_step(NS - 2, 0, 1)
            slot_step(NS - 1, 1, 0)

            for n in range(2):
                act.wait_ge(e_turned, n + 1)
                nc.scalar.activation(YT[n], bank[4 + 2 * n][:, :], ACT.Copy).then_inc(e_evac, 1)

            def weigh(t):
                n, s = real(t), t % 2
                act.wait_ge(d_gather[t], 32)
                if t >= 2:
                    act.wait_ge(moe_set, t - 1)
                nc.scalar.activation(sq_sb[0:n, s * D:(s + 1) * D], qk_sb[0:n, t * D:(t + 1) * D], ACT.Copy,
                                     scale=wt_sb[0:n, 2 * NT + t:2 * NT + t + 1]).then_inc(m1_set, 1)

            def keep_moeT(t):
                s = t % 2
                act.wait_ge(moe_turned, t + 1)
                nc.scalar.activation(xT_sb[:, s * 2 * T:(s + 1) * 2 * T], bank[s][:, 0:2 * T], ACT.Copy).then_inc(moeT_set, 1)

            def gate_exp(t):
                n = real(t)
                act.wait_ge(z_bounded, t + 1)
                nc.scalar.activation(z_sb[0:n, 2 * NT + t:2 * NT + t + 1], z_sb[0:n, NT + t:NT + t + 1], ACT.Exp,
                                     scale=-1.0).then_inc(gexp_set, 1)

            for k in range(NT + 2):
                if k < NT:
                    weigh(k)
                if 1 <= k <= NT:
                    keep_moeT(k - 1)
                if k >= 2:
                    gate_exp(k - 2)

        @block.vector
        def _(dve):
            count = [0]

            def link(ins):
                count[0] += 1
                ins.then_inc(dve_chain, 1)
                dve.wait_ge(dve_chain, count[0])

            for s_ in (h_added_cr, v_kept_cr, ss_set_cr, shifted_cr, pre_kept_cr, hid_biased_cr, ys_set_cr):
                dve.sem_inc(s_, 2)
            dve.sem_inc(s_kept_cr, G)
            dve.sem_inc(att_set_c1, 1)
            dve.sem_inc(h1_added_c1, 1)
            dve.wait_ge(d_con, 48)
            nc.vector.memset(z_sb[:, :], 0.0)
            nc.vector.tensor_copy(idb_sb[0:T, :], identT).then_inc(consts_set, 1)
            nc.vector.tensor_copy(maskb_sb[0:T, :], con_sb[0:T, K_MASK:K_MASK + T]).then_inc(consts_set, 1)
            link(nc.vector.tensor_tensor(row_sb[0:T, R_BASE:R_BASE + D], row_sb[0:T, R_BASE:R_BASE + D], row_sb[0:T, R_POS:R_POS + D], ALU.add))

            def stats(src, t):
                nc.vector.bn_stats(stat_sb[0:T, ds(6 * t, 6)], src[0:T, ds(t * D, D)]).then_inc(stats_done, 1)

            def add_base(t, s):
                dve.wait_ge(embedded, t + 1)
                nc.vector.tensor_tensor(h_sb[0:T, ds(t * D, D)], bank[2 + s][0:T, 0:D], row_sb[0:T, R_BASE:R_BASE + D],
                                        ALU.add).then_inc(h_added_cr, 1)

            def embed_step(t, s):
                dve.wait_ge(h_added_cr, t + 2)
                add_base(t, s)
                stats(h_sb, t - 1)

            add_base(0, 0)
            with dve.Fori(0, 4) as i:
                embed_step(2 * i + 1, 1)
                embed_step(2 * i + 2, 0)
            def aggregate(dst, a, b, before, done):
                for t in range(a, b):
                    dve.wait_ge(stats_done, before + t + 1)
                    nc.vector.bn_aggr(dst[0:T, 2 * t:2 * t + 2], stat_sb[0:T, 6 * t:6 * t + 6]).then_inc(done, 1)

            aggregate(mv_sb, 0, 8, 0, stats1)
            dve.wait_ge(d_qkv, 16)
            for k in range(2):
                w3 = wqkv_sb[:, k * 3 * D:k * 3 * D + 2 * D].rearrange("p (g d) -> p g d", d=HD)
                m = wc_sb[:, k * 2 * NH:(k + 1) * 2 * NH]
                link(nc.vector.tensor_reduce(m, w3, AX.X, ALU.add))
                link(nc.vector.tensor_scalar(m, m, -1.0 / HD, None, ALU.mult))
                nc.vector.tensor_tensor(w3, w3, m.unsqueeze(2).broadcast_to([128, 2 * NH, HD]), ALU.add).then_inc(w_centred, 1)
            for t in range(9, NT):
                embed_step(t, t % 2)
            dve.wait_ge(h_added_cr, NT + 2)
            stats(h_sb, NT - 1)
            aggregate(mv_sb, 8, NT, 0, stats1)

            dve.wait_ge(rstd1, 1)
            dve.wait_ge(half_set, 2)

            def norm_x(t, s):
                nc.vector.tensor_scalar(stage_sb[0:T, s * D:(s + 1) * D], h_sb[0:T, ds(t * D, D)],
                                        mv_sb[0:T, ds(2 * t, 1)], r1_sb[0:T, ds(t, 1)], ALU.subtract, ALU.mult).then_inc(xh_set, 1)

            def qkv_step(t, s, more=True):
                if more:
                    dve.wait_ge(xh_turned, t + 1)
                    norm_x(t + 2, s)
                dve.wait_ge(v_made, t + 1)
                v = v_sb[0:T, ds(t * NH * VW, NH * VW)].rearrange("p (h d) -> p h d", d=VW)
                nc.vector.tensor_copy(v[:, :, 0:HD], bank[2 + s][0:T, 0:D].rearrange("p (h d) -> p h d", d=HD)).then_inc(v_kept_cr, 1)
                dve.wait_ge(qk_squared_cr, t + 3)
                nc.vector.tensor_reduce(ss_sb[0:T, ds(t * 2 * NH, 2 * NH)],
                                        sq_sb[0:T, s * 2 * D:(s + 1) * 2 * D].rearrange("p (g d) -> p g d", d=HD),
                                        AX.X, ALU.add).then_inc(ss_set_cr, 1)

            def variance(n):
                a, b = (0, 8 * 2 * NH) if n == 0 else (8 * 2 * NH, NT * 2 * NH)
                dve.wait_ge(ss_set_cr, (8 if n == 0 else NT) + 2)
                nc.vector.tensor_scalar(ss_sb[0:T, a:b], ss_sb[0:T, a:b], 1.0 / HD, EPS, ALU.mult, ALU.add).then_inc(var_set, 1)

            def newton(n):
                a, b = (0, 8 * 2 * NH) if n == 0 else (8 * 2 * NH, NT * 2 * NH)
                v, r = ss_sb[0:T, a:b], newton_sb[0:T, a:b]
                u = newton_sb[0:T, NT * 2 * NH + a:NT * 2 * NH + b]
                dve.wait_ge(root_set, n + 1)
                link(nc.vector.reciprocal(r, r))
                link(nc.vector.tensor_tensor(u, r, r, ALU.mult))
                link(nc.vector.tensor_tensor(u, u, v, ALU.mult))
                link(nc.vector.tensor_scalar(u, u, -0.5, 1.5, ALU.mult, ALU.add))
                link(nc.vector.tensor_tensor(v, r, u, ALU.mult))

            norm_x(0, 0)
            norm_x(1, 1)
            dve.wait_ge(rstd1, 2)
            pairs(dve, qkv_step, 8)
            variance(0)
            qkv_step(NT - 3, 0)
            newton(0)
            qkv_step(NT - 2, 1, False)
            qkv_step(NT - 1, 0, False)
            variance(1)

            dve.wait_ge(d_zero, 16 * 4)
            dve.wait_ge(hb_set, 1)

            def norm_qk(t, s):
                r = ss_sb[0:T, ds(t * 2 * NH, 2 * NH)].unsqueeze(2).broadcast_to([T, 2 * NH, HD])
                nc.vector.tensor_tensor(qn_sb[0:T, s * 2 * D:(s + 1) * 2 * D].rearrange("p (g d) -> p g d", d=HD),
                                        qk_sb[0:T, ds(t * 2 * D, 2 * D)].rearrange("p (g d) -> p g d", d=HD), r, ALU.mult).then_inc(qn_set, 1)

            def shift(t, s):
                for hf in range(2):
                    dve.wait_ge(scored, 2 * t + hf + 1)
                    for b in range(2):
                        sc = bank[4 + 2 * hf + b][0:T, 0:4 * T].rearrange("p (n m) -> p n m", n=4)
                        h0 = (2 * hf + b) * 4
                        last = nc.vector.tensor_reduce(mx_sb[0:T, h0:h0 + 4], sc, AX.X, ALU.max)
                    last.then_inc(max_set, 1)
                    dve.wait_ge(max_set, 2 * t + hf + 1)
                    for b in range(2):
                        sc = bank[4 + 2 * hf + b][0:T, 0:4 * T].rearrange("p (n m) -> p n m", n=4)
                        h0 = (2 * hf + b) * 4
                        p = p_sb[0:T, (s * NH + h0) * T:(s * NH + h0 + 4) * T].rearrange("p (n m) -> p n m", n=4)
                        last = nc.vector.tensor_tensor(p, sc, mx_sb[0:T, h0:h0 + 4].unsqueeze(2).broadcast_to([T, 4, T]), ALU.subtract)
                    last.then_inc(shifted_cr, 1)

            def add_output(t):
                dve.wait_ge(wo_made, t + 1)
                nc.vector.tensor_tensor(h1_sb[0:T, ds(t * D, D)], bank[3][0:T, 0:D], hb_sb[0:T, ds(t * D, D)],
                                        ALU.add).then_inc(h1_added_c1, 1)

            def attn_step(t, s):
                first = isinstance(t, int) and t < 1
                if not last_tile(t):
                    if not first:
                        dve.wait_ge(turned, 6 * t + 1)
                    shift(t + 1, 1 - s)
                if not first:
                    if not isinstance(t, int) or t >= 2:
                        dve.wait_ge(h1_added_c1, t)
                    add_output(t - 1)
                    if not isinstance(t, int) or t >= 2:
                        stats(h1_sb, t - 2)
                if not isinstance(t, int) or t <= NT - 4:
                    norm_qk(t + 3, 1 - s)
                dve.wait_ge(pv_made, 4 * t + 4)
                pv = bank[2][0:T, 0:NH * VW].rearrange("p (h d) -> p h d", d=VW)
                nc.vector.reciprocal(rc_sb[0:T, :], pv[:, :, HD]).then_inc(rc_set, 1)
                dve.wait_ge(rc_set, t + 1)
                nc.vector.tensor_tensor(att_sb[0:T, s * D:(s + 1) * D].rearrange("p (h d) -> p h d", d=HD), pv[:, :, 0:HD],
                                        rc_sb[0:T, :].unsqueeze(2).broadcast_to([T, NH, HD]), ALU.mult).then_inc(att_set_c1, 1)
                if isinstance(t, int) and t == 8:
                    column_sums()
                if isinstance(t, int) and t == 9:
                    aggregate(mv2_sb, 0, 8, NT, h1_stats)
                    scale_generators()

            def column_sums():
                dve.wait_ge(d_gen, 32)
                link(nc.vector.tensor_reduce(nrm_sb[:, 0:6], aT_sb[:, :].rearrange("p (n c) -> p n c", c=D), AX.X, ALU.add,
                                             apply_absolute_value=True))
                nc.vector.tensor_reduce(nrm_sb[:, 6:7], nrm_sb[:, 0:6], AX.X, ALU.max).then_inc(n_part, 1)

            def scale_generators():
                dve.wait_ge(n_max, 1)
                link(nc.vector.tensor_scalar(nrm_sb[:, 8:9], nrm_sb[:, 7:8], 1.0 / THETA, None, ALU.mult))
                link(nc.vector.tensor_scalar(nrmi_sb[:, 0:1], nrm_sb[:, 8:9].bitcast(i32), 23, None, ALU.logical_shift_right))
                link(nc.vector.tensor_scalar(nrmi_sb[:, 1:2], nrmi_sb[:, 0:1], -126.0, float(SQUARINGS), ALU.add, ALU.max))
                link(nc.vector.tensor_scalar(nrmi_sb[:, 2:3], nrmi_sb[:, 1:2], 20.0, None, ALU.min))
                link(nc.vector.tensor_scalar(nrmi_sb[:, 3:4], nrmi_sb[:, 2:3], -1.0, 127.0, ALU.mult, ALU.add))
                link(nc.vector.tensor_scalar(nrm_sb[:, 9:10].bitcast(i32), nrmi_sb[:, 3:4], 23, None, ALU.logical_shift_left))
                link(nc.vector.tensor_scalar(nrm_sb[:, 10:11], nrm_sb[:, 8:9], EXPM_LIMIT / THETA, 3e38, ALU.is_ge, ALU.mult))
                link(nc.vector.tensor_scalar(nrm_sb[:, 10:11], nrm_sb[:, 10:11], 1e10, None, ALU.mult))
                link(nc.vector.tensor_tensor(nrm_sb[:, 11:12], nrm_sb[:, 10:11], nrm_sb[:, 10:11], ALU.subtract))
                link(nc.vector.tensor_tensor(nrm_sb[:, 12:13], nrm_sb[:, 9:10], nrm_sb[:, 11:12], ALU.add))
                for m in (a_sb, aT_sb[:, :]):
                    nc.vector.tensor_scalar(m, m, nrm_sb[:, 12:13], None, ALU.mult).then_inc(n_scaled, 1)

            norm_qk(0, 0)
            norm_qk(1, 1)
            newton(1)
            shift(0, 0)
            norm_qk(2, 0)
            attn_tiles(dve, attn_step)
            add_output(NT - 1)
            stats(h1_sb, NT - 2)
            dve.wait_ge(h1_added_c1, NT + 1)
            stats(h1_sb, NT - 1)
            aggregate(mv2_sb, 8, NT, NT, h1_stats)

            dve.wait_ge(rstd2, 1)

            def pre_step(t, s):
                h1 = h1_sb[0:T, ds(t * D, D)]
                nc.vector.tensor_scalar(h_sb[0:T, ds(t * D, D)], h1, mv2_sb[0:T, ds(2 * t, 1)], rr_sb[0:T, ds(NT + t, 1)],
                                        ALU.subtract, ALU.mult)
                nc.vector.tensor_scalar(hb_sb[0:T, ds(t * D, D)], h1, rr_sb[0:T, ds(4 * NT + t, 1)], rr_sb[0:T, ds(3 * NT + t, 1)],
                                        ALU.mult, ALU.add)
                dve.wait_ge(pre_made, t + 1)
                nc.vector.tensor_tensor(v_sb[0:T, ds(t * PW, PW)], bank[2 + s][0:T, 0:PW], row_sb[0:T, R_PRE:R_PRE + PW],
                                        ALU.add).then_inc(pre_kept_cr, 1)

            pairs(dve, pre_step, NT - 1)
            pre_step(NT - 1, 0)

            dve.wait_ge(pre_kept_cr, NT + 2)
            for t in range(NT):
                nc.vector.max(top_sb[0:T, t * 8:(t + 1) * 8], v_sb[0:T, t * PW + D:(t + 1) * PW]).then_inc(top_set, 1)
            for t in range(NT):
                dve.wait_ge(top_set, t + 1)
                nc.vector.max_index(idx_sb[0:T, t * 8:(t + 1) * 8], top_sb[0:T, t * 8:(t + 1) * 8],
                                    v_sb[0:T, t * PW + D:(t + 1) * PW]).then_inc(idx_set, 1)
            dve.wait_ge(idx_set, NT)
            top3 = top_sb[0:T].rearrange("p (t k) -> p t k", k=8)
            idx3 = idx_sb[0:T, :].rearrange("p (t k) -> p t k", k=8)
            nc.vector.tensor_tensor(wt_sb[0:T, 0:NT], top3[:, :, 1], top3[:, :, 0], ALU.subtract).then_inc(gap_set, 1)
            L = E * NT
            S = [rt_sb[0:T, n * L:(n + 1) * L] for n in range(8)]
            q = [rt8_sb[0:T, n * E:(n + 1) * E] for n in range(8)]

            def et(ap):
                return ap.rearrange("p (e t) -> p e t", e=E)

            iota_e = con_sb[0:T, K_IOTA:K_IOTA + E]
            for c in range(2):
                ids = S[5][:, 0:NT]
                link(nc.vector.tensor_copy(ids, idx3[:, :, c]))
                link(nc.vector.tensor_tensor(ids, ids, con_sb[0:T, K_INV:K_INV + NT], ALU.add))
                link(nc.vector.tensor_tensor(et(S[c]), iota_e.unsqueeze(2).broadcast_to([T, E, NT]),
                                             ids.unsqueeze(1).broadcast_to([T, E, NT]), ALU.is_equal))
            nc.vector.tensor_tensor(S[2], S[0], S[1], ALU.add).then_inc(onehot_set, 1)
            dve.wait_ge(ranked, 1)
            link(nc.vector.tensor_copy(S[3], bank[1][0:T, 0:L]))
            link(nc.vector.tensor_tensor_scan(S[4], con_sb[0:T, K_SEG:K_SEG + L], S[3], 0.0, ALU.mult, ALU.add))
            link(nc.vector.tensor_tensor(S[5], S[4], S[3], ALU.subtract))
            link(nc.vector.tensor_tensor(S[5], S[5], bank[0][0:T, 0:L], ALU.add))
            ti = rti_sb[0:T, 0:E]
            link(nc.vector.tensor_scalar(ti, et(S[4])[:, :, NT - 1], 127.0, None, ALU.add))
            link(nc.vector.tensor_scalar(ti, ti, 7, None, ALU.logical_shift_right))
            link(nc.vector.tensor_copy(q[0], ti))
            link(nc.vector.tensor_tensor_scan(q[1], con_sb[0:T, K_ONE:K_ONE + E], q[0], 0.0, ALU.mult, ALU.add))
            link(nc.vector.tensor_tensor(q[2], q[1], q[0], ALU.subtract))
            link(nc.vector.tensor_scalar(q[3], q[2], 128.0, None, ALU.mult))
            link(nc.vector.tensor_tensor(et(S[5]), et(S[5]), q[3].unsqueeze(2).broadcast_to([T, E, NT]), ALU.add))
            for c in range(2):
                link(nc.vector.tensor_tensor(S[6], S[5], S[c], ALU.mult))
                link(nc.vector.tensor_reduce(S[7][:, 0:NT], S[6].rearrange("p (e t) -> p t e", e=E), AX.X, ALU.add))
                nc.vector.tensor_copy(slot_sb[0:T, c * NT:(c + 1) * NT], S[7][:, 0:NT]).then_inc(slots_set, 1)
                dve.wait_ge(slots_set, c + 1)
            link(nc.vector.tensor_tensor(cmp_sb[0:T].rearrange("p (j e) -> p j e", e=E),
                                         con_sb[0:T, K_IOTA:K_IOTA + NS].unsqueeze(2).broadcast_to([T, NS, E]),
                                         q[2].unsqueeze(1).broadcast_to([T, NS, E]), ALU.is_ge))
            link(nc.vector.tensor_reduce(ef_sb[0:T], cmp_sb[0:T].rearrange("p (j e) -> p j e", e=E), AX.X, ALU.add))
            nc.vector.tensor_scalar(ei_sb[0:T, :], ef_sb[0:T], -1.0, None, ALU.add).then_inc(experts_set, 1)
            dve.wait_ge(ratio_set, 1)
            link(nc.vector.tensor_scalar(wt_sb[0:T, 2 * NT:3 * NT], wt_sb[0:T, NT:2 * NT], 1.0, None, ALU.add))
            link(nc.vector.reciprocal(wt_sb[0:T, 2 * NT:3 * NT], wt_sb[0:T, 2 * NT:3 * NT]))
            nc.vector.tensor_tensor(wt_sb[0:T, 3 * NT:4 * NT], wt_sb[0:T, NT:2 * NT], wt_sb[0:T, 2 * NT:3 * NT],
                                    ALU.mult).then_inc(resid_set, 1)

            dve.wait_ge(n_scaled, 2)
            c = [1.0]
            for k in range(1, 13):
                c.append(c[-1] / k)
            eye = con_sb[:, K_ID:K_ID + 128]

            def stt(out_, in0, k, in1):
                link(nc.vector.scalar_tensor_tensor(out=out_, in0=in0, scalar=k, in1=in1, op0=ALU.mult, op1=ALU.add))

            def add_eye(x, k):
                d = [x[:, m * D + m * 128:m * D + m * 128 + 128] for m in range(2)]
                stt(d[0], eye, k, d[0])
                nc.vector.scalar_tensor_tensor(out=d[1], in0=eye, scalar=k, in1=d[1], op0=ALU.mult,
                                               op1=ALU.add).then_inc(poly_set, 1)

            for n in range(G):
                dve.wait_ge(x_kept, 2 * G + n + 1)
                link(nc.vector.tensor_scalar(poly[n], A[n], c[9], None, ALU.mult))
                stt(poly[n], A2[n], c[10], poly[n])
                stt(poly[n], A3[n], c[11], poly[n])
                stt(poly[n], A4[n], c[12], poly[n])
                add_eye(poly[n], c[8])
            for n in range(G):
                dve.wait_ge(p_made, n + 1)
                stt(poly[n], A[n], c[5], bank[2 + n][:, :])
                stt(poly[n], A2[n], c[6], poly[n])
                stt(poly[n], A3[n], c[7], poly[n])
                add_eye(poly[n], c[4])
            for n in range(G):
                stt(Y[n], A2[n], c[2], A[n])
                stt(Y[n], A3[n], c[3], Y[n])
                dve.wait_ge(p_made, G + n + 1)
                nc.vector.tensor_tensor(Y[n], Y[n], bank[5 + n][:, :], ALU.add).then_inc(y_set, 1)

            dve.wait_ge(abel_set, 1)
            for t in range(NT):
                link(nc.vector.tensor_tensor_reduce(att_sb[0:T, 0:D], h1_sb[0:T, t * D:(t + 1) * D], row_sb[0:T, R_GW:R_GW + D],
                                                    1.0, row_sb[0:T, R_GCB:R_GCB + 1], ALU.mult, ALU.add, z_sb[0:T, t:t + 1]))

            dve.wait_ge(y_set, G)
            squarings = dve.value_load(nrmi_sb[0:1, 2:3], min_val=SQUARINGS, max_val=20)
            with dve.Fori(0, squarings) as j:
                for n in range(G):
                    dve.wait_ge(s_made, 3 * j + n + 1)
                    nc.vector.scalar_tensor_tensor(out=Y[n], in0=Y[n], scalar=2.0, in1=bank[5 + n][:, :],
                                                   op0=ALU.mult, op1=ALU.add).then_inc(s_kept_cr, 1)

            dve.wait_ge(d_b, 32)
            dve.wait_ge(experts_set, 1)

            def expert_of(j):
                return dve.value_load(ei_sb[0:1, ds(j, 1)], min_val=0, max_val=E - 1)

            def bias_hidden(j, s, e):
                dve.wait_ge(hid_made, j + 1)
                nc.vector.tensor_tensor(hid_sb[:, s * HID:(s + 1) * HID], bank[4 + s][:, :], b1_sb[:, ds(e * HID, HID)],
                                        ALU.add).then_inc(hid_biased_cr, 1)

            def slot_step(j, s, turn, more=True):
                e_next = expert_of(j + 1) if more else None
                e = expert_of(j)
                if more:
                    dve.wait_ge(hid_turned_c1, j + 1)
                    bias_hidden(j + 1, 1 - s, e_next)
                dve.wait_ge(ys_made, j + 1)
                dve.wait_ge(d_ys_c1[s], 16 * turn + 16)
                nc.vector.tensor_tensor(ys_sb[:, s * D:(s + 1) * D], bank[6 + s][:, 0:D], b2_sb[:, ds(e * D, D)],
                                        ALU.add).then_inc(ys_set_cr, 1)

            bias_hidden(0, 0, expert_of(0))
            with dve.Fori(0, NS // 2 - 1) as i:
                slot_step(2 * i, 0, i)
                slot_step(2 * i + 1, 1, i)
            slot_step(NS - 2, 0, NS // 2 - 1)
            slot_step(NS - 1, 1, NS // 2 - 1, False)

            for n in range(2):
                dve.wait_ge(e_made, n + 1)
                link(nc.vector.tensor_tensor(Y[0], Y[0], Y[n + 1], ALU.add))
                nc.vector.tensor_tensor(Y[0], Y[0], bank[5 + 2 * n][:, :], ALU.add).then_inc(e_kept, 1)
                dve.wait_ge(e_kept, n + 1)

            def combine(t):
                n, s = real(t), t % 2
                dve.wait_ge(m1_set, t + 1)
                if t >= 2:
                    dve.wait_ge(moe_turned, t - 1)
                nc.vector.scalar_tensor_tensor(out=qn_sb[0:n, s * D:(s + 1) * D], in0=qk_sb[0:n, (NT + t) * D:(NT + t + 1) * D],
                                               scalar=wt_sb[0:n, 3 * NT + t:3 * NT + t + 1], in1=sq_sb[0:n, s * D:(s + 1) * D],
                                               op0=ALU.mult, op1=ALU.add).then_inc(moe_set, 1)

            def rotated(t):
                n, s = real(t), t % 2
                dve.wait_ge(rot_made, t + 1)
                mo = v_sb[0:n, t * D:(t + 1) * D]
                nc.vector.tensor_tensor(mo, bank[2 + s][0:n, 0:D], qn_sb[0:n, s * D:(s + 1) * D], ALU.add).then_inc(rot_kept, 1)
                dve.wait_ge(rot_kept, t + 1)
                nc.vector.tensor_tensor_reduce(att_sb[0:n, s * D:(s + 1) * D], mo, row_sb[0:n, R_GW + D:R_GW + 2 * D], 1.0,
                                               z_sb[0:n, t:t + 1], ALU.mult, ALU.add, z_sb[0:n, NT + t:NT + t + 1]).then_inc(z_set, 1)
                dve.wait_ge(z_set, t + 1)
                nc.vector.tensor_scalar(z_sb[0:n, NT + t:NT + t + 1], z_sb[0:n, NT + t:NT + t + 1], -87.0, None,
                                        ALU.max).then_inc(z_bounded, 1)

            def result(t):
                n = real(t)
                mo, o = v_sb[0:n, t * D:(t + 1) * D], h1_sb[0:n, t * D:(t + 1) * D]
                g = z_sb[0:n, 3 * NT + t:3 * NT + t + 1]
                nc.vector.tensor_tensor(mo, mo, o, ALU.subtract).then_inc(diff_set, 1)
                dve.wait_ge(gexp_set, t + 1)
                link(nc.vector.tensor_scalar(g, z_sb[0:n, 2 * NT + t:2 * NT + t + 1], 1.0, None, ALU.add))
                link(nc.vector.reciprocal(g, g))
                dve.wait_ge(diff_set, t + 1)
                nc.vector.scalar_tensor_tensor(out=o, in0=mo, scalar=g, in1=hb_sb[0:n, t * D:(t + 1) * D],
                                               op0=ALU.mult, op1=ALU.add).then_inc(out_set, 1)

            dve.wait_ge(abelw_set, 1)
            for k in range(NT + 2):
                if k < NT:
                    combine(k)
                if 1 <= k <= NT:
                    rotated(k - 1)
                if k >= 2:
                    result(k - 2)

        @block.tensor
        def _(pe):
            pe.sem_inc(hid_turned_c1, 1)

            def embed(t, slot, turn):
                pe.wait_ge(d_patch[slot], 16 * (turn + 1))
                pe.wait_ge(h_added_cr, t + 1)
                for k in range(FK):
                    if isinstance(t, int) and t == 0:
                        pe.wait_ge(d_tok[k], 16)
                    last = nc.tensor.matmul(bank[2 + slot % 2][0:T, 0:D], patch_sb[:, (slot * FK + k) * T:(slot * FK + k + 1) * T],
                                            wtok_sb[:, k * D:(k + 1) * D], start=(k == 0), stop=(k == FK - 1))
                last.then_inc(embedded, 1)

            for n in range(3):
                embed(n, n, 0)
            with pe.Fori(0, 2) as i:
                embed(4 * i + 3, 3, i)
                for n in range(3):
                    embed(4 * i + 4 + n, n, i + 1)

            pe.wait_ge(d_con, 48)

            def turn_two(dst, src):
                for c in range(2):
                    last = nc.tensor.transpose(dst[:, c * T:(c + 1) * T], src[:, c * 128:(c + 1) * 128], identT)
                return last

            def turn_x(t, s):
                pe.wait_ge(xh_set, t + 1)
                pe.wait_ge(xT_set_cr, t + 1)
                turn_two(bank[s], stage_sb[0:T, s * D:(s + 1) * D]).then_inc(xh_turned, 1)

            def qkv_step(t, s, more=True):
                if more:
                    turn_x(t + 1, 1 - s)
                pe.wait_ge(xT_set_cr, t + 3)
                pe.wait_ge(qk_squared_cr, t + 1)
                for k in range(2):
                    last = nc.tensor.matmul(bank[4 + s][0:T, :], xT_sb[:, (2 * s + k) * T:(2 * s + k + 1) * T],
                                            wqkv_sb[:, k * 3 * D:k * 3 * D + 2 * D], start=(k == 0), stop=(k == 1))
                last.then_inc(qk_made, 1)
                pe.wait_ge(v_kept_cr, t + 1)
                for k in range(2):
                    last = nc.tensor.matmul(bank[2 + s][0:T, 0:D], xT_sb[:, (2 * s + k) * T:(2 * s + k + 1) * T],
                                            wqkv_sb[:, k * 3 * D + 2 * D:(k + 1) * 3 * D], start=(k == 0), stop=(k == 1))
                last.then_inc(v_made, 1)

            pe.wait_ge(w_centred, 2)
            turn_x(0, 0)
            pairs(pe, qkv_step, NT - 1)
            qkv_step(NT - 1, 0, False)

            pe.wait_ge(consts_set, 2)
            pe.wait_ge(d_w, 32)

            def turn_qk(t, s, u, b):
                pe.wait_ge(qn_set, t + 1)
                pe.wait_ge(evac_cr, u + 1)
                for c in range(4):
                    last = nc.tensor.transpose(bank[b][:, c * T:(c + 1) * T], qn_sb[0:T, s * 2 * D + c * 128:s * 2 * D + (c + 1) * 128], identT)
                last.then_inc(turned, 1)

            mask4 = maskb_sb[0:T, :].unsqueeze(1).broadcast_to([T, 4, T])

            def scores(t, s, evacuated):
                pe.wait_ge(evac_cr, evacuated)
                q0, k0 = s * 6 * T, s * 6 * T + 2 * T
                for hf in range(2):
                    pe.wait_ge(shifted_cr, 2 * t + hf + 1)
                    for r in (2 * hf, 2 * hf + 1):
                        nc.tensor.matmul(bank[4 + r][0:T, 0:4 * T], idb_sb[0:T, :], mask4, start=True, stop=False, skip_group_check=True)
                    for c in range(2):
                        for r in (2 * hf, 2 * hf + 1):
                            last = nc.tensor.matmul(bank[4 + r][0:T, c * 2 * T:(c + 1) * 2 * T],
                                                    qkT_sb[32 * r:32 * r + 32, q0 + c * T:q0 + (c + 1) * T],
                                                    qkT_sb[32 * r:32 * r + 32, k0 + c * 2 * T:k0 + (c + 1) * 2 * T],
                                                    start=False, stop=True, skip_group_check=True)
                    last.then_inc(scored, 1)

            def turn_probs(t, s, g, u, b):
                pe.wait_ge(probs_set, 2 * t + g // 2 + 1)
                pe.wait_ge(evac_cr, u + 1)
                for n in range(4):
                    h0 = (s * NH + 4 * g + n) * T
                    last = nc.tensor.transpose(bank[b][0:T, n * T:(n + 1) * T], p_sb[0:T, h0:h0 + T], identT)
                last.then_inc(turned, 1)

            def values(t, s, g, u, b):
                pe.wait_ge(evac_cr, u + 3)
                if g == 0:
                    pe.wait_ge(att_set_c1, t + 1)
                    pe.wait_ge(v_staged, t + 1)
                for n in range(4):
                    h = 8 * (n // 2) + 2 * g + n % 2
                    v0 = (s * NH + h) * VW
                    last = nc.tensor.matmul(bank[2][0:T, h * VW:(h + 1) * VW], pT_sb[0:T, ((g % 2) * 4 + n) * T:((g % 2) * 4 + n + 1) * T],
                                            keep_v_sb[0:T, v0:v0 + VW], start=True, stop=True, skip_group_check=True)
                last.then_inc(pv_made, 1)

            def turn_att(t, s, u, b):
                pe.wait_ge(att_set_c1, t + 2)
                pe.wait_ge(evac_cr, u + 1)
                turn_two(bank[b], att_sb[0:T, s * D:(s + 1) * D]).then_inc(turned, 1)

            def output(t, u, b):
                pe.wait_ge(evac_cr, u + 3)
                pe.wait_ge(h1_added_c1, t + 1)
                for k in range(2):
                    last = nc.tensor.matmul(bank[3][0:T, 0:D], attT_sb[:, k * T:(k + 1) * T], wo_sb[:, k * D:(k + 1) * D],
                                            start=(k == 0), stop=(k == 1))
                last.then_inc(wo_made, 1)

            def attn_step(t, s):
                u = uses(t)
                if "T" in u:
                    turn_qk(t + 2, s, *u["T"])
                if not last_tile(t):
                    scores(t + 1, 1 - s, 4 if isinstance(t, int) and t == 0 else 6 * t + 3)
                turn_probs(t, s, 0, *u["P0"])
                turn_probs(t, s, 1, *u["P1"])
                if "A" in u:
                    turn_att(t - 1, 1 - s, *u["A"])
                values(t, s, 0, *u["P0"])
                turn_probs(t, s, 2, *u["P2"])
                values(t, s, 1, *u["P1"])
                if "A" in u:
                    output(t - 1, *u["A"])
                turn_probs(t, s, 3, *u["P3"])
                values(t, s, 2, *u["P2"])
                values(t, s, 3, *u["P3"])

            turn_qk(0, 0, 0, 0)
            turn_qk(1, 1, 1, 1)
            scores(0, 0, 3)
            attn_tiles(pe, attn_step)
            turn_att(NT - 1, 0, *LAST_USE)
            output(NT - 1, *LAST_USE)

            def turn_z(t, s):
                pe.wait_ge(zs_set, t + 1)
                pe.wait_ge(zT_set_cr, t + 1)
                turn_two(bank[s], stage_sb[0:T, s * D:(s + 1) * D]).then_inc(z_turned, 1)

            def pre_step(t, s, more=True):
                if more:
                    turn_z(t + 1, 1 - s)
                pe.wait_ge(zT_set_cr, t + 3)
                pe.wait_ge(pre_kept_cr, t + 1)
                for k in range(2):
                    last = nc.tensor.matmul(bank[2 + s][0:T, 0:PW], xT_sb[:, (2 * s + k) * T:(2 * s + k + 1) * T],
                                            wpre_sb[:, k * PW:(k + 1) * PW], start=(k == 0), stop=(k == 1))
                last.then_inc(pre_made, 1)

            turn_z(0, 0)
            pairs(pe, pre_step, NT - 1)
            pre_step(NT - 1, 0, False)

            def rank():
                pe.wait_ge(onehot_set, 1)
                L = E * NT
                for b, k in ((0, K_LOW), (1, K_ONE)):
                    last = nc.tensor.matmul(bank[b][0:T, 0:L], con_sb[0:T, k:k + T], rt_sb[0:T, 2 * L:3 * L], start=True, stop=True)
                last.then_inc(ranked, 1)

            def product(dst, xT, y):
                for m in range(2):
                    for k in range(2):
                        last = nc.tensor.matmul(dst[:, m * D:(m + 1) * D], xT[:, k * D + m * 128:k * D + (m + 1) * 128],
                                                y[:, k * D:(k + 1) * D], start=(k == 0), stop=(k == 1))
                return last

            def turn_square(dst, x):
                for m in range(2):
                    for k in range(2):
                        last = nc.tensor.transpose(dst[:, k * D + m * 128:k * D + (m + 1) * 128],
                                                   x[:, m * D + k * 128:m * D + (k + 1) * 128], ident)
                return last

            pe.wait_ge(n_scaled, 2)
            for n in range(G):
                product(bank[5 + n], AT[n], A[n]).then_inc(x_made, 1)
                if n == 1:
                    rank()
            pe.wait_ge(pre_kept_cr, NT + 2)
            for n in range(G):
                pe.wait_ge(x_kept, n + 1)
                product(bank[2 + n], AT[n], A2[n]).then_inc(x_made, 1)
            for n in range(G):
                pe.wait_ge(x_kept, G + n + 1)
                product(bank[5 + n], AT[n], A3[n]).then_inc(x_made, 1)
            pe.wait_ge(slots_set, 2)
            for n in range(G):
                pe.wait_ge(x_kept, 2 * G + n + 1)
                if n == 2:
                    pe.wait_ge(x_evac, 1)
                turn_square(bank[n % 2], A4[n]).then_inc(x_turned, 1)
            for m in range(2):
                for n in range(G):
                    pe.wait_ge(x_evac, n + 1)
                    pe.wait_ge(poly_set, G * m + n + 1)
                    product(bank[(2, 5)[m] + n], A4T[n], poly[n]).then_inc(p_made, 1)
            pe.wait_ge(y_set, G)
            squarings = pe.value_load(nrmi_sb[0:1, 2:3], min_val=SQUARINGS, max_val=20)
            with pe.Fori(0, squarings) as j:
                for n in range(G):
                    pe.wait_ge(s_kept_cr, 3 * j + n + 1)
                    turn_square(bank[n], Y[n]).then_inc(s_turned, 1)
                for n in range(G):
                    pe.wait_ge(s_evac, 3 * j + n + 1)
                    product(bank[5 + n], YT[n], Y[n]).then_inc(s_made, 1)

            pe.wait_ge(d_exp, 32)
            pe.wait_ge(experts_set, 1)
            pe.wait_ge(s_kept_cr, 3 * squarings + G)

            def turn_xs(j, s, turn):
                pe.wait_ge(d_xs[s], 16 * (turn + 1))
                pe.wait_ge(xsT_set, j)
                for c in range(2):
                    last = nc.tensor.transpose(bank[1][:, c * 128:(c + 1) * 128], xs_sb[:, s * D + c * 128:s * D + (c + 1) * 128], ident)
                last.then_inc(xs_turned, 1)

            def expert_of(j):
                return pe.value_load(ei_sb[0:1, ds(j, 1)], min_val=0, max_val=E - 1)

            def hidden(j, s, e):
                pe.wait_ge(xsT_set, j + 1)
                pe.wait_ge(hid_biased_cr, j + 1)
                for k in range(2):
                    last = nc.tensor.matmul(bank[4 + s][:, :], xsT_sb[:, (2 * s + k) * 128:(2 * s + k + 1) * 128],
                                            w1_sb[:, ds(e * 2 * HID + k * HID, HID)], start=(k == 0), stop=(k == 1))
                last.then_inc(hid_made, 1)

            def slot_step(j, s, turn, e, e_next, ahead=2):
                pe.wait_ge(gelu_set, j + 1)
                pe.wait_ge(hidT_set_c1, j + 1)
                for k in range(4):
                    last = nc.tensor.transpose(bank[0][:, k * 128:(k + 1) * 128], hid_sb[:, s * HID + k * 128:s * HID + (k + 1) * 128], ident)
                last.then_inc(hid_turned_c1, 1)
                if ahead == 2:
                    turn_xs(j + 2, s, turn + 1)
                if ahead >= 1:
                    hidden(j + 1, 1 - s, e_next)
                pe.wait_ge(hidT_set_c1, j + 2)
                pe.wait_ge(ys_set_cr, j + 1)
                for k in range(4):
                    last = nc.tensor.matmul(bank[6 + s][:, 0:D], hidT_sb[:, k * 128:(k + 1) * 128],
                                            w2_sb[:, ds(e * 4 * D + k * D, D)], start=(k == 0), stop=(k == 3))
                last.then_inc(ys_made, 1)

            turn_xs(0, 0, 0)
            hidden(0, 0, expert_of(0))
            turn_xs(1, 1, 0)
            with pe.Fori(0, NS // 2 - 1) as i:
                e = [expert_of(2 * i + n) for n in range(3)]
                slot_step(2 * i, 0, i, e[0], e[1])
                slot_step(2 * i + 1, 1, i, e[1], e[2])
            e = [expert_of(NS - 2 + n) for n in range(2)]
            slot_step(NS - 2, 0, None, e[0], e[1], 1)
            slot_step(NS - 1, 1, None, e[1], None, 0)

            pe.wait_ge(hid_biased_cr, NS + 2)
            pe.wait_ge(ys_set_cr, NS + 2)
            for n in range(2):
                if n:
                    pe.wait_ge(e_kept, n)
                turn_square(bank[4 + 2 * n], Y[0]).then_inc(e_turned, 1)
                pe.wait_ge(e_evac, n + 1)
                product(bank[5 + 2 * n], YT[n], Y[n + 1]).then_inc(e_made, 1)
            pe.wait_ge(e_kept, 2)

            def turn_moe(t):
                n, s = (T if t < NT - 1 else TLAST), t % 2
                pe.wait_ge(moe_set, t + 1)
                if t >= 2:
                    pe.wait_ge(moeT_set, t - 1)
                for c in range(2):
                    last = nc.tensor.transpose(bank[s][:, c * T:c * T + n], qn_sb[0:n, s * D + c * 128:s * D + (c + 1) * 128], con_sb[0:n, K_ID:K_ID + n])
                last.then_inc(moe_turned, 1)

            def rotate(t):
                n, s = (T if t < NT - 1 else TLAST), t % 2
                pe.wait_ge(moeT_set, t + 1)
                if t >= 2:
                    pe.wait_ge(rot_kept, t - 1)
                for k in range(2):
                    last = nc.tensor.matmul(bank[2 + s][0:n, 0:D], xT_sb[:, (2 * s + k) * T:(2 * s + k) * T + n],
                                            y_sb[:, k * D:(k + 1) * D], start=(k == 0), stop=(k == 1))
                last.then_inc(rot_made, 1)

            turn_moe(0)
            for t in range(1, NT):
                turn_moe(t)
                rotate(t - 1)
            rotate(NT - 1)


def _rows_to_partitions(a):
    a = np.asarray(a)
    k = a.shape[-2] // 128
    a = a.reshape(a.shape[:-2] + (k, 128, a.shape[-1]))
    return np.ascontiguousarray(np.moveaxis(a, -2, 0)).reshape(128, -1)


def _constants():
    con = np.zeros((128, NCONST), np.float32)
    p = np.arange(128)
    con[:, K_ID:K_ID + 128] = np.eye(128)
    q, m = np.meshgrid(np.arange(T), np.arange(T), indexing="ij")
    con[:T, K_MASK:K_MASK + T] = np.where((q // SEQ == m // SEQ) & (m <= q), 0.0, NEG)
    con[:, K_LOW:K_LOW + 128] = p[:, None] < p[None, :]
    con[:, K_ONE:K_ONE + 128] = 1.0
    con[:, K_IOTA:K_IOTA + 32] = np.arange(32)
    con[TLAST:, K_INV + NT - 1] = 100.0
    con[:, K_SEG:K_SEG + E * NT] = (np.arange(E * NT) % NT != 0)
    return con


def kernel(x, cls_tok, L0_tok_w, L0_tok_b, L0_tok_cls_token, L0_tok_pos, L0_attn_mask, L0_attn_Wq, L0_attn_Wk, L0_attn_Wv,
           L0_attn_gq, L0_attn_bq, L0_attn_gk, L0_attn_bk, L0_attn_Wo, L0_attn_bo, L0_ffn_ln_gamma, L0_ffn_ln_beta,
           L0_ffn_abel_w, L0_ffn_abel_b, L0_ffn_moe_gate_w, L0_ffn_moe_gate_b, L0_ffn_ew1, L0_ffn_eb1, L0_ffn_ew2,
           L0_ffn_eb2, L0_ffn_gens, L0_ffn_gc_w, L0_ffn_gc_b):
    import concourse.bacc as bacc
    from concourse.bass_utils import run_bass_kernel_spmd

    f32 = np.float32
    P = 16
    x = np.asarray(x)
    C, W = x.shape[1], x.shape[2] // P
    patches = x.reshape(B, C, W, P, W, P).transpose(0, 2, 4, 1, 3, 5).reshape(B, W * W, C * P * P)
    tok = np.zeros((NT * IPT, SEQ, C * P * P), f32)
    tok[:B, 2:] = patches
    tok = tok.reshape(NT, T, FK, 128).transpose(0, 3, 2, 1).reshape(NT, 128, FK * T)

    cols = np.zeros((128, NCOL), f32)
    even = (np.arange(128) // HD) % 2 == 0
    cols[:, C_GQ], cols[:, C_BQ] = np.tile(L0_attn_gq, 8), np.tile(L0_attn_bq, 8)
    for j, mine in enumerate((even, ~even)):
        cols[mine, C_GK + j] = np.tile(L0_attn_gk, 8)[mine]
        cols[mine, C_BK + j] = np.tile(L0_attn_bk, 8)[mine]
    cols[:, C_GAM:C_GAM + 2] = np.asarray(L0_ffn_ln_gamma).reshape(2, 128).T
    cols[:, C_BET:C_BET + 2] = np.asarray(L0_ffn_ln_beta).reshape(2, 128).T

    rows = np.zeros((128, NROW), f32)
    for n in range(IPT):
        r = n * SEQ
        rows[r, R_BASE:R_BASE + D] = np.asarray(cls_tok).reshape(D)
        rows[r + 1, R_BASE:R_BASE + D] = L0_tok_cls_token
        rows[r + 2:r + SEQ, R_BASE:R_BASE + D] = L0_tok_b
        rows[r + 1:r + SEQ, R_POS:R_POS + D] = L0_tok_pos
    rows[:, R_BO:R_BO + D] = L0_attn_bo
    rows[:, R_PRE:R_PRE + D] = L0_ffn_abel_b
    rows[:, R_PRE + D:R_PRE + PW] = L0_ffn_moe_gate_b
    rows[:, R_GW:R_GW + 2 * D] = np.asarray(L0_ffn_gc_w).reshape(2 * D)
    rows[:, R_GCB] = np.asarray(L0_ffn_gc_b)

    gens = np.asarray(L0_ffn_gens)
    arrays = {
        "patches": tok,
        "w_tok": _rows_to_partitions(np.asarray(L0_tok_w).T),
        "w_qkv": _rows_to_partitions(np.concatenate([L0_attn_Wq, L0_attn_Wk, L0_attn_Wv]).T),
        "w_o": _rows_to_partitions(np.asarray(L0_attn_Wo).T),
        "w_pre": _rows_to_partitions(np.concatenate([L0_ffn_abel_w, L0_ffn_moe_gate_w], axis=1)),
        "w1": _rows_to_partitions(L0_ffn_ew1),
        "w2": _rows_to_partitions(L0_ffn_ew2),
        "b1": np.asarray(L0_ffn_eb1).reshape(1, E * HID),
        "b2": np.asarray(L0_ffn_eb2).reshape(1, E * D),
        "gens": _rows_to_partitions(gens),
        "gens_t": _rows_to_partitions(gens.transpose(0, 2, 1)),
        "cols": cols, "rows": rows, "consts": _constants(),
    }
    nc = bacc.Bacc("TRN2", target_bir_lowering=False, num_devices=1)
    arrays = {f"in_{k}": np.ascontiguousarray(v) for k, v in arrays.items()}
    args = [nc.dram_tensor(k, v.shape, mybir.dt.from_np(v.dtype), kind="ExternalInput").ap() for k, v in arrays.items()]
    out = nc.dram_tensor("out_rows", (B * SEQ, D), mybir.dt.float32, kind="ExternalOutput").ap()
    vit_kernel(nc, *args, out)
    r = run_bass_kernel_spmd(nc, [arrays], core_ids=[0])
    return r.results[0]["out_rows"].reshape(B, SEQ, D)
```

```python
from contextlib import ExitStack

import concourse.bass as bass
import numpy as np
from concourse import mybir

B, SEQ, D = 32, 38, 256
IPT = 3
T = IPT * SEQ
NT = -(-B // IPT)
TLAST = B * SEQ - (NT - 1) * T
FK = 6
NH, HD = 16, 16
VW = HD + 1
E, HID = 8, 512
NS = (2 * B * SEQ + E * 127) // 128
PW = D + E
EPS = 1e-5
NEG = -1e30
G = 3
SQUARINGS = 4
THETA = 1.7
EXPM_LIMIT = 3.925724783138660 * 2.0 ** 17

C_GAM, C_BET = 0, 2
NCOL = 4
R_BASE, R_POS, R_BO, R_PRE, R_GW, R_GCB = 0, D, 2 * D, 3 * D, 3 * D + PW, 5 * D + PW
R_QK = R_GCB + 1
NROW = R_QK + 4 * HD
K_ID, K_MASK, K_LOW, K_ONE, K_IOTA, K_INV, K_SEG = 0, 128, 256, 384, 512, 544, 566
NCONST = 654


def vit_kernel(nc, patches, w_tok, w_qkv, w_o, w_pre, w1, w2, b1, b2, gens, gens_t,
               cols, rows, consts, out):
    f32r = mybir.dt.float32r
    fp32, bf16, i32, u32 = mybir.dt.float32, mybir.dt.bfloat16, mybir.dt.int32, mybir.dt.uint32
    ALU, ACT, AX = mybir.AluOpType, mybir.ActivationFunctionType, mybir.AxisListType
    ds = bass.ds
    ctx = ExitStack()
    with ctx:
        def sb(name, width, dt=fp32):
            return ctx.enter_context(nc.sbuf_tensor(name, [128, width], dt))

        def sem(name):
            return ctx.enter_context(nc.semaphore(name))

        xs_dram = nc.dram_tensor("xs_rows", (NS * 128, D), fp32, kind="Internal").ap()
        ys_dram = nc.dram_tensor("ys_rows", (NS * 128, D), fp32, kind="Internal").ap()

        patch_sb = sb("patch_sb", 4 * FK * T)
        wtok_sb = sb("wtok_sb", FK * D)
        wqkv_sb = sb("wqkv_sb", 2 * 3 * D)
        wo_sb = sb("wo_sb", 2 * D)
        w1_sb = sb("w1_sb", E * 2 * HID)
        with ExitStack() as early:
            def early_sb(name, width, dt):
                return early.enter_context(nc.sbuf_tensor(name, [128, width], dt))

            parts_sb = early_sb("parts_sb", 2 * 8 * D, f32r)
            qkT_sb = early_sb("qkT_sb", 2 * 24 * T, f32r)
            ident_r = early_sb("ident_r", T, f32r)
        w2_sb = sb("w2_sb", E * 4 * D)
        spare_sb = sb("spare_sb", 2 * 512)
        wpre_sb = sb("wpre_sb", 2 * PW)
        col_sb = sb("col_sb", NCOL)
        row_sb = sb("row_sb", NROW)
        con_sb = sb("con_sb", NCONST)
        idb_sb = sb("idb_sb", T, bf16)
        maskb_sb = sb("maskb_sb", T, bf16)
        h_sb = sb("h_sb", NT * D)
        hb_sb = sb("hb_sb", NT * D)
        h1_sb = sb("h1_sb", NT * D)
        qk_sb = sb("qk_sb", NT * 2 * D)
        v_sb = sb("v_sb", NT * NH * VW)
        stage_sb = sb("stage_sb", 2 * D)
        xT_sb = sb("xT_sb", 2 * 2 * T)
        sq_sb = sb("sq_sb", 2 * 2 * D)
        qn_sb = sb("qn_sb", 2 * 2 * D)
        p_sb = sb("p_sb", 2 * NH * T)
        pT_sb = sb("pT_sb", 2 * 4 * T)
        att_sb = sb("att_sb", 2 * D)
        attT_sb = sb("attT_sb", 2 * T)
        mv_sb = sb("mv_sb", 2 * NT)
        mv2_sb = sb("mv2_sb", 2 * NT)
        ss_sb = sb("ss_sb", NT * 2 * NH)
        half_sb = sb("half_sb", 1)
        r1_sb = sb("r1_sb", NT)
        rr_sb = sb("rr_sb", 6 * NT)
        mx_sb = sb("mx_sb", NH)
        rc_sb = sb("rc_sb", NH)
        idx_sb = sb("idx_sb", NT * 8, u32)
        rti_sb = sb("rti_sb", E, i32)
        ei_sb = sb("ei_sb", NS, i32)
        slot_sb = sb("slot_sb", 2 * NT, i32)
        wt_sb = sb("wt_sb", 4 * NT)
        z_sb = sb("z_sb", 4 * NT)
        nrm_sb = sb("nrm_sb", 16)
        nrmi_sb = sb("nrmi_sb", 4, i32)

        def tri(t_, k, w):
            return t_[0:T, ds(k * w, w)]

        b2_sb = p_sb[:, 0:E * D]
        y_sb = p_sb[:, E * D:E * D + G * 512]
        yT_sb = wtok_sb
        b1_sb = qk_sb[:, 0:E * HID]
        a_sb, aT_sb = patch_sb[:, 0:G * 512], wqkv_sb
        keep_v_sb = sq_sb[:, 0:2 * NH * VW]
        newton_sb = p_sb[:, 0:2 * NT * 2 * NH]
        gain_sb, shift_sb = wtok_sb[:, 0:2 * D], wtok_sb[:, 2 * D:4 * D]

        def parts(s, k, low):
            at = (2 * s + k) * 4 * D
            p = parts_sb[0:T, at:at + 4 * D]
            if k == 0:
                return p.rearrange("p (h a b d) -> p h a b d", a=2, b=2, d=HD)[:, :, low, :, :]
            return p.rearrange("p (h a b d) -> p h a b d", a=2, b=2, d=HD)[:, :, :, low, :]

        def normed(s, k):
            at = (2 * s + k) * D
            return qn_sb[0:T, at:at + D].rearrange("p (h d) -> p h d", d=HD).unsqueeze(2).broadcast_to([T, NH, 2, HD])

        A2 = [qk_sb[:, n * 512:(n + 1) * 512] for n in range(G)]
        A3 = [qk_sb[:, (3 + n) * 512:(4 + n) * 512] for n in range(G)]
        A4 = [qk_sb[:, (6 + n) * 512:(7 + n) * 512] for n in range(G)]
        poly = [qk_sb[:, 9 * 512:10 * 512], qk_sb[:, 10 * 512:11 * 512], spare_sb[:, 0:512]]
        A4T = [spare_sb[:, 512:1024], sq_sb[:, 0:512], sq_sb[:, 512:1024]]
        A = [a_sb[:, n * 512:(n + 1) * 512] for n in range(G)]
        AT = [aT_sb[:, n * 512:(n + 1) * 512] for n in range(G)]
        Y = [y_sb[:, n * 512:(n + 1) * 512] for n in range(G)]
        YT = [yT_sb[:, n * 512:(n + 1) * 512] for n in range(G)]
        hid_sb, hidT_sb = sq_sb, stage_sb
        zero_sb = h1_sb[:, 0:NS * D // 4]
        rt_sb = sq_sb[:, 0:8 * E * NT]
        cmp_sb = pT_sb[:, 0:NS * E]
        wc_sb = pT_sb[:, 256:256 + 4 * NH]
        rt8_sb = pT_sb[:, 320:320 + 8 * E]
        ef_sb = pT_sb[:, 384:384 + NS]
        top_sb = att_sb[:, 0:NT * 8]
        stat_sb = idx_sb[:, 0:NT * 6].bitcast(fp32)
        xs_sb, xsT_sb = qn_sb[:, 0:2 * D], qn_sb[:, 2 * D:4 * D]
        ys_sb = pT_sb

        bank = [ctx.enter_context(nc.psum_tensor(f"bank{n}", [128, 512], fp32)) for n in range(8)]

        d_tok = [sem(f"d_tok{k}") for k in range(FK)]
        d_con, d_qkv, d_w, d_exp = sem("d_con"), sem("d_qkv"), sem("d_w"), sem("d_exp")
        d_pre, low_k_set, k_cleared = sem("d_pre"), sem("low_k_set"), sem("k_cleared")
        d_patch = [sem(f"d_patch{n}") for n in range(4)]
        d_zero, d_b, d_gen, d_scat = sem("d_zero"), sem("d_b"), sem("d_gen"), sem("d_scat")
        d_xs = [sem("d_xs0"), sem("d_xs1")]
        d_ys_c1 = [sem("d_ys0_c1"), sem("d_ys1_c1")]
        d_gather = [sem(f"d_gather{n}") for n in range(NT)]
        d_out = sem("d_out")
        consts_set, zero_set, half_set = sem("consts_set"), sem("zero_set"), sem("half_set")
        dve_chain, pool_chain = sem("dve_chain"), sem("pool_chain")
        embedded, h_added_cr = sem("embedded"), sem("h_added_cr")
        stats1, rstd1, hb_set = sem("stats1"), sem("rstd1"), sem("hb_set")
        w_centred, xh_set, xh_turned, xT_set_cr = sem("w_centred"), sem("xh_set"), sem("xh_turned"), sem("xT_set_cr")
        qk_made, v_made, qk_squared_cr, v_kept_cr, ss_set_cr = (
            sem("qk_made"), sem("v_made"), sem("qk_squared_cr"), sem("v_kept_cr"), sem("ss_set_cr"))
        rstd_qk = sem("rstd_qk")
        qn_set, turned, evac_cr = sem("qn_set"), sem("turned"), sem("evac_cr")
        gains_set, scaled_set, affine_set, high_set, low_set, idr_set = (
            sem("gains_set"), sem("scaled_set"), sem("affine_set"), sem("high_set"), sem("low_set"), sem("idr_set"))
        scored, shifted_cr, max_set, probs_set = sem("scored"), sem("shifted_cr"), sem("max_set"), sem("probs_set")
        pv_made, rc_set, att_set_c1, wo_made, h1_added_c1 = (
            sem("pv_made"), sem("rc_set"), sem("att_set"), sem("wo_made"), sem("h1_added"))
        h1_stats, rstd2 = sem("h1_stats"), sem("rstd2")
        zs_set, z_turned, zT_set_cr, pre_made, pre_kept_cr = (
            sem("zs_set"), sem("z_turned"), sem("zT_set_cr"), sem("pre_made"), sem("pre_kept_cr"))
        top_set, idx_set, abel_set = sem("top_set"), sem("idx_set"), sem("abel_set")
        onehot_set, ranked, slots_set, experts_set = sem("onehot_set"), sem("ranked"), sem("slots_set"), sem("experts_set")
        gap_set, ratio_set, resid_set, abelw_set = sem("gap_set"), sem("ratio_set"), sem("resid_set"), sem("abelw_set")
        n_part, n_max, n_scaled, v_staged = sem("n_part"), sem("n_max"), sem("n_scaled"), sem("v_staged")
        x_made, x_kept, x_turned, x_evac, p_made, y_set = (
            sem("x_made"), sem("x_kept"), sem("x_turned"), sem("x_evac"), sem("p_made"), sem("y_set"))
        var_set, root_set = sem("var_set"), sem("root_set")
        z_bounded = sem("z_bounded")
        poly_set, stats_done = sem("poly_set"), sem("stats_done")
        s_made, s_kept_cr, s_turned, s_evac = sem("s_made"), sem("s_kept_cr"), sem("s_turned"), sem("s_evac")
        e_made, e_kept, e_turned, e_evac = sem("e_made"), sem("e_kept"), sem("e_turned"), sem("e_evac")
        xs_turned, xsT_set, hid_made, hid_biased_cr, gelu_set = (
            sem("xs_turned"), sem("xsT_set"), sem("hid_made"), sem("hid_biased_cr"), sem("gelu_set"))
        hid_turned_c1, hidT_set_c1, ys_made, ys_set_cr = sem("hid_turned_c1"), sem("hidT_set_c1"), sem("ys_made"), sem("ys_set_cr")
        m1_set, moe_set, moe_turned, moeT_set, rot_made, rot_kept, z_set = (
            sem("m1_set"), sem("moe_set"), sem("moe_turned"), sem("moeT_set"), sem("rot_made"), sem("rot_kept"), sem("z_set"))
        gexp_set, gate_set, diff_set, out_set = sem("gexp_set"), sem("gate_set"), sem("diff_set"), sem("out_set")

        ident = con_sb[:, K_ID:K_ID + 128]
        identT = con_sb[0:T, K_ID:K_ID + T]

        def col(c):
            return col_sb[:, c:c + 1]

        def pairs(eng, step, n):
            with eng.Fori(0, n // 2) as i:
                step(2 * i, 0)
                step(2 * i + 1, 1)

        QK = ["Q0", "Q1", "K0", "K1"]

        def names_of(t):
            known = isinstance(t, int)
            return (QK if not known or t <= NT - 3 else []) + ["P0", "P1"] + (["A"] if not known or t > 0 else []) + ["P2", "P3"]

        def first_use(t):
            if isinstance(t, int):
                return 8 + sum(len(names_of(n)) for n in range(t))
            return 9 * t + 7

        def uses(t, s):
            odd = first_use(t) % 2 if isinstance(t, int) else (s + 1) % 2
            return {name: (first_use(t) + n, (odd + n) % 2) for n, name in enumerate(names_of(t))}

        LAST_USE = (first_use(NT), first_use(NT) % 2)

        def real(t):
            return T if t < NT - 1 else TLAST

        def last_tile(t):
            return isinstance(t, int) and t == NT - 1

        def attn_tiles(eng, step):
            step(0, 0)
            with eng.Fori(0, 3) as i:
                step(2 * i + 1, 1)
                step(2 * i + 2, 0)
            for t in range(7, NT):
                step(t, t % 2)

        EARLY = 4

        block = ctx.enter_context(nc.Block())

        @block.sync
        def _(sp):
            sp.sem_inc(d_ys_c1[0], 16)
            sp.sem_inc(d_ys_c1[1], 16)
            sp.dma_start(patch_sb[:, 0:FK * T], patches[0]).then_inc(d_patch[0], 16)
            for k in range(FK):
                sp.dma_start(wtok_sb[:, k * D:(k + 1) * D], w_tok[:, k * D:(k + 1) * D]).then_inc(d_tok[k], 16)
            for t in range(1, 4):
                sp.dma_start(patch_sb[:, t * FK * T:(t + 1) * FK * T], patches[t]).then_inc(d_patch[t], 16)
            sp.dma_start(con_sb[:, :], consts).then_inc(d_con, 16)
            sp.dma_start(wqkv_sb[:, :], w_qkv).then_inc(d_qkv, 16)
            for t in range(4, NT):
                sp.wait_ge(embedded, t - 3)
                s = t % 4
                sp.dma_start(patch_sb[:, s * FK * T:(s + 1) * FK * T], patches[t]).then_inc(d_patch[s], 16)
            sp.dma_start(wo_sb[:, :], w_o).then_inc(d_w, 16)
            sp.wait_ge(zero_set, 1)
            zview = xs_dram.rearrange("(p a) d -> p (a d)", p=128)
            ZW = NS * D // 4
            for n in range(4):
                sp.dma_start(zview[:, n * ZW:(n + 1) * ZW], zero_sb).then_inc(d_zero, 16)
            sp.dma_start(w1_sb[:, :], w1).then_inc(d_exp, 16)
            sp.wait_ge(embedded, NT)
            sp.dma_start(a_sb, gens).then_inc(d_gen, 16)
            sp.wait_ge(v_made, NT)
            sp.dma_start(aT_sb[:, :], gens_t).then_inc(d_gen, 16)
            sp.wait_ge(scored, 2 * NT)
            sp.dma_start(wpre_sb[:, :], w_pre).then_inc(d_pre, 16)
            sp.dma_start(w2_sb[:, :], w2).then_inc(d_exp, 16)
            sp.wait_ge(h1_added_c1, NT + 1)
            sp.dma_start(b2_sb, b2.broadcast_to([128, E * D])).then_inc(d_b, 16)

            def load(j, s):
                sp.dma_start(xs_sb[:, s * D:(s + 1) * D], xs_dram[ds(j * 128, 128), :]).then_inc(d_xs[s], 16)

            def store(j, s):
                sp.wait_ge(ys_set_cr, j + 3)
                sp.dma_start(ys_dram[ds(j * 128, 128), :], ys_sb[:, s * D:(s + 1) * D]).then_inc(d_ys_c1[s], 16)

            def slot_step(j, s):
                sp.wait_ge(xs_turned, j + 3)
                load(j + 4, s)
                store(j, s)

            sp.wait_ge(d_scat, 16 * 2 * NT)
            load(0, 0)
            load(1, 1)
            sp.wait_ge(y_set, G)
            sp.dma_start(b1_sb, b1.broadcast_to([128, E * HID])).then_inc(d_b, 16)
            for j in range(2):
                sp.wait_ge(xs_turned, j + 1)
                load(j + 2, j)
            pairs(sp, slot_step, NS - 4)
            for j in range(NS - 4, NS):
                store(j, j % 2)

            def out_tile(t):
                sp.wait_ge(out_set, t + 1)
                sp.dma_start(out[ds(t * T, T), :], h1_sb[0:T, ds(t * D, D)]).then_inc(d_out, 16)

            with sp.Fori(0, NT - 1) as t:
                out_tile(t)
            sp.wait_ge(out_set, NT)
            sp.dma_start(out[(NT - 1) * T:B * SEQ, :], h1_sb[0:TLAST, (NT - 1) * D:NT * D]).then_inc(d_out, 16)
            sp.wait_ge(d_out, 16 * NT)

        @block.gpsimd
        def _(pool):
            count = [0]

            def link(ins):
                count[0] += 1
                ins.then_inc(pool_chain, 1)
                pool.wait_ge(pool_chain, count[0])

            pool.memset(zero_sb, 0.0).then_inc(zero_set, 1)
            pool.memset(half_sb[:, :], -0.5).then_inc(half_set, 1)
            pool.memset(v_sb[:, :], 1.0).then_inc(half_set, 1)
            pool.wait_ge(half_set, 2)
            pool.wait_ge(zero_set, 1)
            for s in range(2):
                k0 = (24 * s + 8) * T
                pool.tensor_copy(qkT_sb[:, k0:k0 + 16 * T], zero_sb[:, 0:1].broadcast_to([128, 16 * T])).then_inc(k_cleared, 1)

            def rstd_of(a, b, count):
                pool.wait_ge(stats1, count)
                var1 = mv_sb[0:T, 2 * a:2 * b].rearrange("p (t c) -> p t c", c=2)[:, :, 1]
                link(pool.tensor_scalar(r1_sb[0:T, a:b], var1, EPS, None, ALU.add))
                pool.tensor_tensor(r1_sb[0:T, a:b], r1_sb[0:T, a:b], half_sb[0:T, :].broadcast_to([T, b - a]),
                                   ALU.pow).then_inc(rstd1, 1)

            rstd_of(0, 8, 8)
            rstd_of(8, NT, NT)
            for n in range(2):
                for at, dst in ((R_QK, gain_sb), (R_QK + 2 * HD, shift_sb)):
                    v = row_sb[0:T, at + n * HD:at + (n + 1) * HD].unsqueeze(1).broadcast_to([T, NH, HD])
                    pool.tensor_copy(dst[0:T, n * D:(n + 1) * D].rearrange("p (h d) -> p h d", d=HD), v).then_inc(gains_set, 1)
            pool.wait_ge(gains_set, 4)

            def affine(t, s):
                qk = qn_sb[0:T, s * 2 * D:(s + 1) * 2 * D]
                pool.wait_ge(qn_set, t + 1)
                pool.tensor_tensor(qk, qk, gain_sb[0:T, :], ALU.mult).then_inc(scaled_set, 1)
                pool.wait_ge(scaled_set, t + 1)
                pool.tensor_tensor(qk, qk, shift_sb[0:T, :], ALU.add).then_inc(affine_set, 1)

            def stage_v(t, s):
                pool.tensor_copy(keep_v_sb[0:T, s * NH * VW:(s + 1) * NH * VW], v_sb[0:T, ds(t * NH * VW, NH * VW)]).then_inc(v_staged, 1)

            def low_k(t, s):
                pool.wait_ge(high_set, t + 1)
                pool.tensor_tensor(parts(s, 1, 1), normed(s, 1), parts(s, 1, 0), ALU.subtract).then_inc(low_k_set, 1)

            def pool_step(t, s):
                if not isinstance(t, int) or t <= NT - 5:
                    affine(t + 4, s)
                if not isinstance(t, int) or t <= NT - 4:
                    low_k(t + 3, 1 - s)
                pool.wait_ge(pv_made, 4 * t + 4)
                stage_v(t + 2, s)

            affine(0, 0)
            affine(1, 1)
            low_k(0, 0)
            low_k(1, 1)
            affine(2, 0)
            affine(3, 1)
            bo = row_sb[0:T, R_BO:R_BO + D].unsqueeze(1).broadcast_to([T, NT, D])
            pool.tensor_tensor(hb_sb[0:T, :].rearrange("p (t d) -> p t d", d=D),
                               h_sb[0:T, :].rearrange("p (t d) -> p t d", d=D), bo, ALU.add).then_inc(hb_set, 1)
            low_k(2, 0)
            pool.wait_ge(ss_set_cr, NT + 2)
            stage_v(0, 0)
            stage_v(1, 1)
            pool_step(0, 0)
            with pool.Fori(0, 3) as i:
                pool_step(2 * i + 1, 1)
                pool_step(2 * i + 2, 0)
            pool_step(7, 1)
            pool.wait_ge(n_part, 1)
            pool.partition_all_reduce(nrm_sb[:, 7:8], nrm_sb[:, 6:7], 128, bass.bass_isa.ReduceOp.max).then_inc(n_max, 1)
            pool_step(8, 0)

            def rstd_pair(a, b, count):
                pool.wait_ge(h1_stats, count)
                v2 = mv2_sb[0:T, 2 * a:2 * b].rearrange("p (t c) -> p t c", c=2)[:, :, 1]
                m2 = mv2_sb[0:T, 2 * a:2 * b].rearrange("p (t c) -> p t c", c=2)[:, :, 0]
                half = half_sb[0:T, :].broadcast_to([T, b - a])
                R = [rr_sb[0:T, n * NT + a:n * NT + b] for n in range(5)]
                link(pool.tensor_scalar(R[0], v2, EPS, None, ALU.add))
                link(pool.tensor_scalar(R[1], R[0], EPS, None, ALU.mult))
                link(pool.tensor_tensor(R[1], R[1], v2, ALU.add))
                link(pool.tensor_tensor(R[0], R[0], half, ALU.pow))
                link(pool.tensor_tensor(R[1], R[1], half, ALU.pow))
                link(pool.tensor_tensor(R[2], m2, R[1], ALU.mult))
                link(pool.tensor_scalar(R[2], R[2], -1.0, None, ALU.mult))
                link(pool.tensor_tensor(R[3], m2, R[0], ALU.mult))
                link(pool.tensor_scalar(R[3], R[3], -1.0, None, ALU.mult))
                pool.tensor_scalar(R[4], R[0], 1.0, None, ALU.add).then_inc(rstd2, 1)

            rstd_pair(0, 8, 8)
            rstd_pair(8, NT, NT)
            pool.wait_ge(d_zero, 16 * 4)
            pool.wait_ge(slots_set, 2)
            for t in range(NT):
                n = T if t < NT - 1 else TLAST
                for c in range(2):
                    pool.indirect_dma_start(
                        out=xs_dram, out_offset=bass.IndirectOffsetOnAxis(ap=slot_sb[0:n, c * NT + t:c * NT + t + 1].bitcast(u32), axis=0),
                        in_=h_sb[0:n, t * D:(t + 1) * D], in_offset=None).then_inc(d_scat, 16)
            pool.wait_ge(abel_set, 1)
            pool.wait_ge(resid_set, 1)
            ab3 = h1_sb[0:T, :].rearrange("p (t d) -> p t d", d=D)
            hb3 = hb_sb[0:T, :].rearrange("p (t d) -> p t d", d=D)
            pool.tensor_tensor(hb3, hb3, ab3, ALU.add).then_inc(abelw_set, 1)
            pool.wait_ge(d_ys_c1[0], 16 * (NS // 2 + 1))
            pool.wait_ge(d_ys_c1[1], 16 * (NS // 2 + 1))
            for t in range(NT):
                n = T if t < NT - 1 else TLAST
                for c in range(2):
                    pool.indirect_dma_start(
                        out=qk_sb[0:n, (c * NT + t) * D:(c * NT + t + 1) * D], out_offset=None, in_=ys_dram,
                        in_offset=bass.IndirectOffsetOnAxis(ap=slot_sb[0:n, c * NT + t:c * NT + t + 1].bitcast(u32), axis=0)).then_inc(d_gather[t], 16)

        @block.scalar
        def _(act):
            act.dma_start(row_sb[:, :], rows).then_inc(d_con, 16)
            act.dma_start(col_sb[:, :], cols).then_inc(d_con, 16)
            act.sem_inc(xT_set_cr, 2)
            act.sem_inc(qk_squared_cr, 2)
            act.sem_inc(evac_cr, 2)
            act.sem_inc(zT_set_cr, 2)
            act.sem_inc(hidT_set_c1, 1)

            def keep_xT(t, s):
                act.wait_ge(xh_turned, t + 1)
                nc.scalar.activation(xT_sb[:, s * 2 * T:(s + 1) * 2 * T], bank[s][:, 0:2 * T], ACT.Copy).then_inc(xT_set_cr, 1)

            def qkv_step(t, s, more=True):
                if more:
                    keep_xT(t + 1, 1 - s)
                act.wait_ge(qk_made, t + 1)
                nc.scalar.activation(qk_sb[0:T, ds(t * 2 * D, 2 * D)], bank[4 + s][0:T, :], ACT.Copy)
                act.wait_ge(ss_set_cr, t + 1)
                nc.scalar.activation(sq_sb[0:T, s * 2 * D:(s + 1) * 2 * D], bank[4 + s][0:T, :], ACT.Square).then_inc(qk_squared_cr, 1)

            def high(t, s):
                act.wait_ge(affine_set, t + 1)
                nc.scalar.activation(parts(s, 0, 0), normed(s, 0), ACT.Copy)
                nc.scalar.activation(parts(s, 1, 0), normed(s, 1), ACT.Copy).then_inc(high_set, 1)

            act.wait_ge(d_con, 48)
            keep_xT(0, 0)
            def root(n):
                a, b = (0, EARLY * 2 * NH) if n == 0 else (EARLY * 2 * NH, NT * 2 * NH)
                act.wait_ge(var_set, n + 1)
                nc.scalar.activation(newton_sb[0:T, a:b], ss_sb[0:T, a:b], ACT.Sqrt).then_inc(root_set, 1)

            pairs(act, qkv_step, EARLY)
            root(0)
            for t in range(EARLY, NT):
                if t in (6, 8):
                    high(t // 2 - 3, t // 2 - 3)
                qkv_step(t, t % 2, t < NT - 1)
            root(1)

            def keep_qkT(u, s, b, quarter):
                act.wait_ge(turned, u + 1)
                if quarter < 2:
                    q0 = (24 * s + 4 * quarter) * T
                    last = nc.scalar.activation(qkT_sb[:, q0:q0 + 4 * T], bank[b][:, 0:4 * T].bitcast(f32r), ACT.Copy)
                else:
                    k0 = (24 * s + 8 + 8 * (quarter - 2)) * T
                    for j in range(2):
                        rows = slice(64 * j, 64 * j + 64)
                        last = nc.scalar.activation(
                            qkT_sb[rows, k0:k0 + 8 * T].rearrange("p (n j m) -> p n j m", j=2, m=T)[:, :, j, :],
                            bank[b][rows, 0:4 * T].bitcast(f32r).rearrange("p (n m) -> p n m", m=T), ACT.Copy)
                last.then_inc(evac_cr, 1)

            def exp_half(t, s, hf):
                act.wait_ge(shifted_cr, 2 * t + hf + 3)
                p = p_sb[0:T, (s * NH + hf * 8) * T:(s * NH + hf * 8 + 8) * T]
                nc.scalar.activation(p, p, ACT.Exp).then_inc(probs_set, 1)

            def keep_pT(u, b, g):
                act.wait_ge(turned, u + 1)
                nc.scalar.activation(pT_sb[0:T, (g % 2) * 4 * T:(g % 2 + 1) * 4 * T], bank[b][0:T, 0:4 * T], ACT.Copy).then_inc(evac_cr, 1)

            def keep_attT(u, b):
                act.wait_ge(turned, u + 1)
                nc.scalar.activation(attT_sb[:, :], bank[b][:, 0:2 * T], ACT.Copy).then_inc(evac_cr, 1)

            def attn_step(t, s):
                u = uses(t, s)
                if not isinstance(t, int) or t <= NT - 4:
                    high(t + 3, 1 - s)
                for n, name in enumerate(QK):
                    if name in u:
                        keep_qkT(u[name][0], s, u[name][1], n)
                keep_pT(*u["P0"], 0)
                keep_pT(*u["P1"], 1)
                if "A" in u:
                    keep_attT(*u["A"])
                keep_pT(*u["P2"], 2)
                keep_pT(*u["P3"], 3)
                if not last_tile(t):
                    exp_half(t + 1, 1 - s, 0)
                    exp_half(t + 1, 1 - s, 1)

            act.wait_ge(idr_set, 1)
            act.wait_ge(k_cleared, 2)
            for t in range(2):
                for n in range(4):
                    keep_qkT(4 * t + n, t, n % 2, n)
                if t == 0:
                    high(2, 0)
            exp_half(0, 0, 0)
            exp_half(0, 0, 1)
            attn_tiles(act, attn_step)
            keep_attT(*LAST_USE)

            act.wait_ge(rstd2, 1)

            def stage_z(t, s):
                nc.scalar.activation(stage_sb[0:T, s * D:(s + 1) * D], h1_sb[0:T, ds(t * D, D)], ACT.Identity,
                                     scale=rr_sb[0:T, ds(NT + t, 1)], bias=rr_sb[0:T, ds(2 * NT + t, 1)]).then_inc(zs_set, 1)

            def keep_zT(t, s):
                act.wait_ge(z_turned, t + 1)
                for c in range(2):
                    last = nc.scalar.activation(xT_sb[:, (2 * s + c) * T:(2 * s + c + 1) * T], bank[s][:, c * T:(c + 1) * T],
                                                ACT.Identity, scale=col(C_GAM + c), bias=col(C_BET + c))
                last.then_inc(zT_set_cr, 1)

            def pre_step(t, s, ahead=2):
                if ahead == 2:
                    act.wait_ge(z_turned, t + 1)
                    stage_z(t + 2, s)
                if ahead >= 1:
                    keep_zT(t + 1, 1 - s)

            stage_z(0, 0)
            stage_z(1, 1)
            keep_zT(0, 0)
            act.wait_ge(rstd2, 2)
            pairs(act, pre_step, NT - 3)
            pre_step(NT - 3, 0)
            pre_step(NT - 2, 1, 1)
            act.wait_ge(gap_set, 1)
            nc.scalar.activation(wt_sb[0:T, NT:2 * NT], wt_sb[0:T, 0:NT], ACT.Exp).then_inc(ratio_set, 1)
            act.wait_ge(pre_kept_cr, NT + 2)
            nc.scalar.activation(h1_sb[0:T, :].rearrange("p (t d) -> p t d", d=D),
                                 v_sb[0:T, 0:NT * PW].rearrange("p (t d) -> p t d", d=PW)[:, :, 0:D], ACT.Gelu).then_inc(abel_set, 1)
            x = 0
            for dst, b0 in ((A2, 5), (A3, 2), (A4, 5)):
                for n in range(G):
                    x += 1
                    act.wait_ge(x_made, x)
                    nc.scalar.activation(dst[n], bank[b0 + n][:, :], ACT.Copy).then_inc(x_kept, 1)
            act.wait_ge(slots_set, 2)
            for n in range(G):
                act.wait_ge(x_turned, n + 1)
                nc.scalar.activation(A4T[n], bank[n % 2][:, :], ACT.Copy).then_inc(x_evac, 1)
            squarings = act.value_load(nrmi_sb[0:1, 2:3], min_val=SQUARINGS, max_val=20)
            with act.Fori(0, squarings) as j:
                for n in range(G):
                    act.wait_ge(s_turned, 3 * j + n + 1)
                    nc.scalar.activation(YT[n], bank[n][:, :], ACT.Copy).then_inc(s_evac, 1)

            def keep_xsT(j, s):
                act.wait_ge(xs_turned, j + 1)
                for c in range(2):
                    last = nc.scalar.activation(xsT_sb[:, (2 * s + c) * 128:(2 * s + c + 1) * 128], bank[1][:, c * 128:(c + 1) * 128],
                                                ACT.Identity, scale=col(C_GAM + c), bias=col(C_BET + c))
                last.then_inc(xsT_set, 1)

            def gelu(j, s):
                act.wait_ge(hid_biased_cr, j + 3)
                hid = hid_sb[:, s * HID:(s + 1) * HID]
                nc.scalar.activation(hid, hid, ACT.Gelu).then_inc(gelu_set, 1)

            def slot_step(j, s, ahead=2):
                act.wait_ge(hid_turned_c1, j + 2)
                nc.scalar.activation(hidT_sb[:, :], bank[0][:, :], ACT.Copy).then_inc(hidT_set_c1, 1)
                if ahead == 2:
                    keep_xsT(j + 2, s)
                if ahead >= 1:
                    gelu(j + 1, 1 - s)

            keep_xsT(0, 0)
            keep_xsT(1, 1)
            gelu(0, 0)
            pairs(act, slot_step, NS - 2)
            slot_step(NS - 2, 0, 1)
            slot_step(NS - 1, 1, 0)

            for n in range(2):
                act.wait_ge(e_turned, n + 1)
                nc.scalar.activation(YT[n], bank[4 + 2 * n][:, :], ACT.Copy).then_inc(e_evac, 1)

            def weigh(t):
                n, s = real(t), t % 2
                act.wait_ge(d_gather[t], 32)
                if t >= 2:
                    act.wait_ge(moe_set, t - 1)
                nc.scalar.activation(sq_sb[0:n, s * D:(s + 1) * D], qk_sb[0:n, t * D:(t + 1) * D], ACT.Copy,
                                     scale=wt_sb[0:n, 2 * NT + t:2 * NT + t + 1]).then_inc(m1_set, 1)

            def keep_moeT(t):
                s = t % 2
                act.wait_ge(moe_turned, t + 1)
                nc.scalar.activation(xT_sb[:, s * 2 * T:(s + 1) * 2 * T], bank[s][:, 0:2 * T], ACT.Copy).then_inc(moeT_set, 1)

            def gate_exp(t):
                n = real(t)
                act.wait_ge(z_bounded, t + 1)
                nc.scalar.activation(z_sb[0:n, 2 * NT + t:2 * NT + t + 1], z_sb[0:n, NT + t:NT + t + 1], ACT.Exp,
                                     scale=-1.0).then_inc(gexp_set, 1)

            for k in range(NT + 2):
                if k < NT:
                    weigh(k)
                if 1 <= k <= NT:
                    keep_moeT(k - 1)
                if k >= 2:
                    gate_exp(k - 2)

        @block.vector
        def _(dve):
            count = [0]

            def link(ins):
                count[0] += 1
                ins.then_inc(dve_chain, 1)
                dve.wait_ge(dve_chain, count[0])

            for s_ in (h_added_cr, v_kept_cr, ss_set_cr, shifted_cr, pre_kept_cr, hid_biased_cr, ys_set_cr):
                dve.sem_inc(s_, 2)
            dve.sem_inc(s_kept_cr, G)
            dve.sem_inc(att_set_c1, 1)
            dve.sem_inc(h1_added_c1, 1)
            dve.wait_ge(d_con, 48)
            nc.vector.memset(z_sb[:, :], 0.0)
            nc.vector.tensor_copy(ident_r[0:T, :], identT).then_inc(idr_set, 1)
            nc.vector.tensor_copy(idb_sb[0:T, :], identT).then_inc(consts_set, 1)
            nc.vector.tensor_copy(maskb_sb[0:T, :], con_sb[0:T, K_MASK:K_MASK + T]).then_inc(consts_set, 1)
            link(nc.vector.tensor_tensor(row_sb[0:T, R_BASE:R_BASE + D], row_sb[0:T, R_BASE:R_BASE + D], row_sb[0:T, R_POS:R_POS + D], ALU.add))

            def stats(src, t):
                nc.vector.bn_stats(stat_sb[0:T, ds(6 * t, 6)], src[0:T, ds(t * D, D)]).then_inc(stats_done, 1)

            def add_base(t, s):
                dve.wait_ge(embedded, t + 1)
                nc.vector.tensor_tensor(h_sb[0:T, ds(t * D, D)], bank[2 + s][0:T, 0:D], row_sb[0:T, R_BASE:R_BASE + D],
                                        ALU.add).then_inc(h_added_cr, 1)

            def embed_step(t, s):
                dve.wait_ge(h_added_cr, t + 2)
                add_base(t, s)
                stats(h_sb, t - 1)

            add_base(0, 0)
            with dve.Fori(0, 4) as i:
                embed_step(2 * i + 1, 1)
                embed_step(2 * i + 2, 0)
            def aggregate(dst, a, b, before, done):
                for t in range(a, b):
                    dve.wait_ge(stats_done, before + t + 1)
                    nc.vector.bn_aggr(dst[0:T, 2 * t:2 * t + 2], stat_sb[0:T, 6 * t:6 * t + 6]).then_inc(done, 1)

            aggregate(mv_sb, 0, 8, 0, stats1)
            dve.wait_ge(d_qkv, 16)
            for k in range(2):
                w3 = wqkv_sb[:, k * 3 * D:k * 3 * D + 2 * D].rearrange("p (g d) -> p g d", d=HD)
                m = wc_sb[:, k * 2 * NH:(k + 1) * 2 * NH]
                link(nc.vector.tensor_reduce(m, w3, AX.X, ALU.add))
                link(nc.vector.tensor_scalar(m, m, -1.0 / HD, None, ALU.mult))
                nc.vector.tensor_tensor(w3, w3, m.unsqueeze(2).broadcast_to([128, 2 * NH, HD]), ALU.add).then_inc(w_centred, 1)
            for t in range(9, NT):
                embed_step(t, t % 2)
            dve.wait_ge(h_added_cr, NT + 2)
            stats(h_sb, NT - 1)
            aggregate(mv_sb, 8, NT, 0, stats1)

            dve.wait_ge(rstd1, 1)
            dve.wait_ge(half_set, 2)

            def norm_x(t, s):
                nc.vector.tensor_scalar(stage_sb[0:T, s * D:(s + 1) * D], h_sb[0:T, ds(t * D, D)],
                                        mv_sb[0:T, ds(2 * t, 1)], r1_sb[0:T, ds(t, 1)], ALU.subtract, ALU.mult).then_inc(xh_set, 1)

            def qkv_step(t, s, more=True):
                if more:
                    dve.wait_ge(xh_turned, t + 1)
                    norm_x(t + 2, s)
                dve.wait_ge(v_made, t + 1)
                v = v_sb[0:T, ds(t * NH * VW, NH * VW)].rearrange("p (h d) -> p h d", d=VW)
                nc.vector.tensor_copy(v[:, :, 0:HD], bank[2 + s][0:T, 0:D].rearrange("p (h d) -> p h d", d=HD)).then_inc(v_kept_cr, 1)
                dve.wait_ge(qk_squared_cr, t + 3)
                nc.vector.tensor_reduce(ss_sb[0:T, ds(t * 2 * NH, 2 * NH)],
                                        sq_sb[0:T, s * 2 * D:(s + 1) * 2 * D].rearrange("p (g d) -> p g d", d=HD),
                                        AX.X, ALU.add).then_inc(ss_set_cr, 1)

            def variance(n):
                a, b = (0, EARLY * 2 * NH) if n == 0 else (EARLY * 2 * NH, NT * 2 * NH)
                dve.wait_ge(ss_set_cr, (EARLY if n == 0 else NT) + 2)
                nc.vector.tensor_scalar(ss_sb[0:T, a:b], ss_sb[0:T, a:b], 1.0 / HD, EPS, ALU.mult, ALU.add).then_inc(var_set, 1)

            def newton(n):
                a, b = (0, EARLY * 2 * NH) if n == 0 else (EARLY * 2 * NH, NT * 2 * NH)
                v, r = ss_sb[0:T, a:b], newton_sb[0:T, a:b]
                u = newton_sb[0:T, NT * 2 * NH + a:NT * 2 * NH + b]
                dve.wait_ge(root_set, n + 1)
                link(nc.vector.reciprocal(r, r))
                link(nc.vector.tensor_tensor(u, r, r, ALU.mult))
                link(nc.vector.tensor_tensor(u, u, v, ALU.mult))
                link(nc.vector.tensor_scalar(u, u, -0.5, 1.5, ALU.mult, ALU.add))
                link(nc.vector.tensor_tensor(v, r, u, ALU.mult))

            norm_x(0, 0)
            norm_x(1, 1)
            dve.wait_ge(rstd1, 2)
            def norm_qk(t, s):
                if not isinstance(t, int) or t >= 2:
                    dve.wait_ge(low_set, t - 1)
                    dve.wait_ge(low_k_set, t - 1)
                r = ss_sb[0:T, ds(t * 2 * NH, 2 * NH)].unsqueeze(2).broadcast_to([T, 2 * NH, HD])
                nc.vector.tensor_tensor(qn_sb[0:T, s * 2 * D:(s + 1) * 2 * D].rearrange("p (g d) -> p g d", d=HD),
                                        qk_sb[0:T, ds(t * 2 * D, 2 * D)].rearrange("p (g d) -> p g d", d=HD), r, ALU.mult).then_inc(qn_set, 1)

            def low(t, s):
                dve.wait_ge(high_set, t + 1)
                nc.vector.tensor_tensor(parts(s, 0, 1), normed(s, 0), parts(s, 0, 0), ALU.subtract).then_inc(low_set, 1)

            pairs(dve, qkv_step, EARLY)
            variance(0)
            for t in range(EARLY, NT):
                qkv_step(t, t % 2, t < NT - 2)
                if t == 4:
                    newton(0)
                    norm_qk(0, 0)
                    norm_qk(1, 1)
                elif t in (6, 8):
                    low(t // 2 - 3, t // 2 - 3)
                    norm_qk(t // 2 - 1, t // 2 - 3)
            variance(1)

            dve.wait_ge(d_zero, 16 * 4)
            dve.wait_ge(hb_set, 1)

            def shift(t, s):
                for hf in range(2):
                    dve.wait_ge(scored, 2 * t + hf + 1)
                    for b in range(2):
                        sc = bank[4 + 2 * hf + b][0:T, 0:4 * T].rearrange("p (n m) -> p n m", n=4)
                        h0 = (2 * hf + b) * 4
                        last = nc.vector.tensor_reduce(mx_sb[0:T, h0:h0 + 4], sc, AX.X, ALU.max)
                    last.then_inc(max_set, 1)
                    dve.wait_ge(max_set, 2 * t + hf + 1)
                    for b in range(2):
                        sc = bank[4 + 2 * hf + b][0:T, 0:4 * T].rearrange("p (n m) -> p n m", n=4)
                        h0 = (2 * hf + b) * 4
                        p = p_sb[0:T, (s * NH + h0) * T:(s * NH + h0 + 4) * T].rearrange("p (n m) -> p n m", n=4)
                        last = nc.vector.tensor_tensor(p, sc, mx_sb[0:T, h0:h0 + 4].unsqueeze(2).broadcast_to([T, 4, T]), ALU.subtract)
                    last.then_inc(shifted_cr, 1)

            def add_output(t):
                dve.wait_ge(wo_made, t + 1)
                nc.vector.tensor_tensor(h1_sb[0:T, ds(t * D, D)], bank[3][0:T, 0:D], hb_sb[0:T, ds(t * D, D)],
                                        ALU.add).then_inc(h1_added_c1, 1)

            def attn_step(t, s):
                first = isinstance(t, int) and t < 1
                if not last_tile(t):
                    if not first:
                        dve.wait_ge(turned, first_use(t))
                    shift(t + 1, 1 - s)
                if not first:
                    add_output(t - 1)
                if not isinstance(t, int) or t <= NT - 5:
                    norm_qk(t + 4, s)
                if not first:
                    dve.wait_ge(h1_added_c1, t + 1)
                if not isinstance(t, int) or t <= NT - 4:
                    low(t + 3, 1 - s)
                if not first:
                    stats(h1_sb, t - 1)
                dve.wait_ge(pv_made, 4 * t + 4)
                pv = bank[2][0:T, 0:NH * VW].rearrange("p (h d) -> p h d", d=VW)
                nc.vector.reciprocal(rc_sb[0:T, :], pv[:, :, HD]).then_inc(rc_set, 1)
                dve.wait_ge(rc_set, t + 1)
                nc.vector.tensor_tensor(att_sb[0:T, s * D:(s + 1) * D].rearrange("p (h d) -> p h d", d=HD), pv[:, :, 0:HD],
                                        rc_sb[0:T, :].unsqueeze(2).broadcast_to([T, NH, HD]), ALU.mult).then_inc(att_set_c1, 1)
                if isinstance(t, int) and t == 8:
                    column_sums()
                if isinstance(t, int) and t == 9:
                    aggregate(mv2_sb, 0, 8, NT, h1_stats)
                    scale_generators()

            def column_sums():
                dve.wait_ge(d_gen, 32)
                link(nc.vector.tensor_reduce(nrm_sb[:, 0:6], aT_sb[:, :].rearrange("p (n c) -> p n c", c=D), AX.X, ALU.add,
                                             apply_absolute_value=True))
                nc.vector.tensor_reduce(nrm_sb[:, 6:7], nrm_sb[:, 0:6], AX.X, ALU.max).then_inc(n_part, 1)

            def scale_generators():
                dve.wait_ge(n_max, 1)
                link(nc.vector.tensor_scalar(nrm_sb[:, 8:9], nrm_sb[:, 7:8], 1.0 / THETA, None, ALU.mult))
                link(nc.vector.tensor_scalar(nrmi_sb[:, 0:1], nrm_sb[:, 8:9].bitcast(i32), 23, None, ALU.logical_shift_right))
                link(nc.vector.tensor_scalar(nrmi_sb[:, 1:2], nrmi_sb[:, 0:1], -126.0, float(SQUARINGS), ALU.add, ALU.max))
                link(nc.vector.tensor_scalar(nrmi_sb[:, 2:3], nrmi_sb[:, 1:2], 20.0, None, ALU.min))
                link(nc.vector.tensor_scalar(nrmi_sb[:, 3:4], nrmi_sb[:, 2:3], -1.0, 127.0, ALU.mult, ALU.add))
                link(nc.vector.tensor_scalar(nrm_sb[:, 9:10].bitcast(i32), nrmi_sb[:, 3:4], 23, None, ALU.logical_shift_left))
                link(nc.vector.tensor_scalar(nrm_sb[:, 10:11], nrm_sb[:, 8:9], EXPM_LIMIT / THETA, 3e38, ALU.is_ge, ALU.mult))
                link(nc.vector.tensor_scalar(nrm_sb[:, 10:11], nrm_sb[:, 10:11], 1e10, None, ALU.mult))
                link(nc.vector.tensor_tensor(nrm_sb[:, 11:12], nrm_sb[:, 10:11], nrm_sb[:, 10:11], ALU.subtract))
                link(nc.vector.tensor_tensor(nrm_sb[:, 12:13], nrm_sb[:, 9:10], nrm_sb[:, 11:12], ALU.add))
                for m in (a_sb, aT_sb[:, :]):
                    nc.vector.tensor_scalar(m, m, nrm_sb[:, 12:13], None, ALU.mult).then_inc(n_scaled, 1)

            newton(1)
            low(2, 0)
            shift(0, 0)
            attn_tiles(dve, attn_step)
            add_output(NT - 1)
            dve.wait_ge(h1_added_c1, NT + 1)
            stats(h1_sb, NT - 1)
            aggregate(mv2_sb, 8, NT, NT, h1_stats)

            dve.wait_ge(rstd2, 1)

            def pre_step(t, s):
                h1 = h1_sb[0:T, ds(t * D, D)]
                nc.vector.tensor_scalar(h_sb[0:T, ds(t * D, D)], h1, mv2_sb[0:T, ds(2 * t, 1)], rr_sb[0:T, ds(NT + t, 1)],
                                        ALU.subtract, ALU.mult)
                nc.vector.tensor_scalar(hb_sb[0:T, ds(t * D, D)], h1, rr_sb[0:T, ds(4 * NT + t, 1)], rr_sb[0:T, ds(3 * NT + t, 1)],
                                        ALU.mult, ALU.add)
                dve.wait_ge(pre_made, t + 1)
                nc.vector.tensor_tensor(v_sb[0:T, ds(t * PW, PW)], bank[2 + s][0:T, 0:PW], row_sb[0:T, R_PRE:R_PRE + PW],
                                        ALU.add).then_inc(pre_kept_cr, 1)

            pairs(dve, pre_step, NT - 1)
            pre_step(NT - 1, 0)

            dve.wait_ge(pre_kept_cr, NT + 2)
            for t in range(NT):
                nc.vector.max(top_sb[0:T, t * 8:(t + 1) * 8], v_sb[0:T, t * PW + D:(t + 1) * PW]).then_inc(top_set, 1)
            for t in range(NT):
                dve.wait_ge(top_set, t + 1)
                nc.vector.max_index(idx_sb[0:T, t * 8:(t + 1) * 8], top_sb[0:T, t * 8:(t + 1) * 8],
                                    v_sb[0:T, t * PW + D:(t + 1) * PW]).then_inc(idx_set, 1)
            dve.wait_ge(idx_set, NT)
            top3 = top_sb[0:T].rearrange("p (t k) -> p t k", k=8)
            idx3 = idx_sb[0:T, :].rearrange("p (t k) -> p t k", k=8)
            nc.vector.tensor_tensor(wt_sb[0:T, 0:NT], top3[:, :, 1], top3[:, :, 0], ALU.subtract).then_inc(gap_set, 1)
            L = E * NT
            S = [rt_sb[0:T, n * L:(n + 1) * L] for n in range(8)]
            q = [rt8_sb[0:T, n * E:(n + 1) * E] for n in range(8)]

            def et(ap):
                return ap.rearrange("p (e t) -> p e t", e=E)

            iota_e = con_sb[0:T, K_IOTA:K_IOTA + E]
            for c in range(2):
                ids = S[5][:, 0:NT]
                link(nc.vector.tensor_copy(ids, idx3[:, :, c]))
                link(nc.vector.tensor_tensor(ids, ids, con_sb[0:T, K_INV:K_INV + NT], ALU.add))
                link(nc.vector.tensor_tensor(et(S[c]), iota_e.unsqueeze(2).broadcast_to([T, E, NT]),
                                             ids.unsqueeze(1).broadcast_to([T, E, NT]), ALU.is_equal))
            nc.vector.tensor_tensor(S[2], S[0], S[1], ALU.add).then_inc(onehot_set, 1)
            dve.wait_ge(ranked, 1)
            link(nc.vector.tensor_copy(S[3], bank[1][0:T, 0:L]))
            link(nc.vector.tensor_tensor_scan(S[4], con_sb[0:T, K_SEG:K_SEG + L], S[3], 0.0, ALU.mult, ALU.add))
            link(nc.vector.tensor_tensor(S[5], S[4], S[3], ALU.subtract))
            link(nc.vector.tensor_tensor(S[5], S[5], bank[0][0:T, 0:L], ALU.add))
            ti = rti_sb[0:T, 0:E]
            link(nc.vector.tensor_scalar(ti, et(S[4])[:, :, NT - 1], 127.0, None, ALU.add))
            link(nc.vector.tensor_scalar(ti, ti, 7, None, ALU.logical_shift_right))
            link(nc.vector.tensor_copy(q[0], ti))
            link(nc.vector.tensor_tensor_scan(q[1], con_sb[0:T, K_ONE:K_ONE + E], q[0], 0.0, ALU.mult, ALU.add))
            link(nc.vector.tensor_tensor(q[2], q[1], q[0], ALU.subtract))
            link(nc.vector.tensor_scalar(q[3], q[2], 128.0, None, ALU.mult))
            link(nc.vector.tensor_tensor(et(S[5]), et(S[5]), q[3].unsqueeze(2).broadcast_to([T, E, NT]), ALU.add))
            for c in range(2):
                link(nc.vector.tensor_tensor(S[6], S[5], S[c], ALU.mult))
                link(nc.vector.tensor_reduce(S[7][:, 0:NT], S[6].rearrange("p (e t) -> p t e", e=E), AX.X, ALU.add))
                nc.vector.tensor_copy(slot_sb[0:T, c * NT:(c + 1) * NT], S[7][:, 0:NT]).then_inc(slots_set, 1)
                dve.wait_ge(slots_set, c + 1)
            link(nc.vector.tensor_tensor(cmp_sb[0:T].rearrange("p (j e) -> p j e", e=E),
                                         con_sb[0:T, K_IOTA:K_IOTA + NS].unsqueeze(2).broadcast_to([T, NS, E]),
                                         q[2].unsqueeze(1).broadcast_to([T, NS, E]), ALU.is_ge))
            link(nc.vector.tensor_reduce(ef_sb[0:T], cmp_sb[0:T].rearrange("p (j e) -> p j e", e=E), AX.X, ALU.add))
            nc.vector.tensor_scalar(ei_sb[0:T, :], ef_sb[0:T], -1.0, None, ALU.add).then_inc(experts_set, 1)
            dve.wait_ge(ratio_set, 1)
            link(nc.vector.tensor_scalar(wt_sb[0:T, 2 * NT:3 * NT], wt_sb[0:T, NT:2 * NT], 1.0, None, ALU.add))
            link(nc.vector.reciprocal(wt_sb[0:T, 2 * NT:3 * NT], wt_sb[0:T, 2 * NT:3 * NT]))
            nc.vector.tensor_tensor(wt_sb[0:T, 3 * NT:4 * NT], wt_sb[0:T, NT:2 * NT], wt_sb[0:T, 2 * NT:3 * NT],
                                    ALU.mult).then_inc(resid_set, 1)

            dve.wait_ge(n_scaled, 2)
            c = [1.0]
            for k in range(1, 13):
                c.append(c[-1] / k)
            eye = con_sb[:, K_ID:K_ID + 128]

            def stt(out_, in0, k, in1):
                link(nc.vector.scalar_tensor_tensor(out=out_, in0=in0, scalar=k, in1=in1, op0=ALU.mult, op1=ALU.add))

            def add_eye(x, k):
                d = [x[:, m * D + m * 128:m * D + m * 128 + 128] for m in range(2)]
                stt(d[0], eye, k, d[0])
                nc.vector.scalar_tensor_tensor(out=d[1], in0=eye, scalar=k, in1=d[1], op0=ALU.mult,
                                               op1=ALU.add).then_inc(poly_set, 1)

            for n in range(G):
                dve.wait_ge(x_kept, 2 * G + n + 1)
                link(nc.vector.tensor_scalar(poly[n], A[n], c[9], None, ALU.mult))
                stt(poly[n], A2[n], c[10], poly[n])
                stt(poly[n], A3[n], c[11], poly[n])
                stt(poly[n], A4[n], c[12], poly[n])
                add_eye(poly[n], c[8])
            for n in range(G):
                dve.wait_ge(p_made, n + 1)
                stt(poly[n], A[n], c[5], bank[2 + n][:, :])
                stt(poly[n], A2[n], c[6], poly[n])
                stt(poly[n], A3[n], c[7], poly[n])
                add_eye(poly[n], c[4])
            for n in range(G):
                stt(Y[n], A2[n], c[2], A[n])
                stt(Y[n], A3[n], c[3], Y[n])
                dve.wait_ge(p_made, G + n + 1)
                nc.vector.tensor_tensor(Y[n], Y[n], bank[5 + n][:, :], ALU.add).then_inc(y_set, 1)

            dve.wait_ge(abel_set, 1)
            for t in range(NT):
                link(nc.vector.tensor_tensor_reduce(att_sb[0:T, 0:D], h1_sb[0:T, t * D:(t + 1) * D], row_sb[0:T, R_GW:R_GW + D],
                                                    1.0, row_sb[0:T, R_GCB:R_GCB + 1], ALU.mult, ALU.add, z_sb[0:T, t:t + 1]))

            dve.wait_ge(y_set, G)
            squarings = dve.value_load(nrmi_sb[0:1, 2:3], min_val=SQUARINGS, max_val=20)
            with dve.Fori(0, squarings) as j:
                for n in range(G):
                    dve.wait_ge(s_made, 3 * j + n + 1)
                    nc.vector.scalar_tensor_tensor(out=Y[n], in0=Y[n], scalar=2.0, in1=bank[5 + n][:, :],
                                                   op0=ALU.mult, op1=ALU.add).then_inc(s_kept_cr, 1)

            dve.wait_ge(d_b, 32)
            dve.wait_ge(experts_set, 1)

            def expert_of(j):
                return dve.value_load(ei_sb[0:1, ds(j, 1)], min_val=0, max_val=E - 1)

            def bias_hidden(j, s, e):
                dve.wait_ge(hid_made, j + 1)
                nc.vector.tensor_tensor(hid_sb[:, s * HID:(s + 1) * HID], bank[4 + s][:, :], b1_sb[:, ds(e * HID, HID)],
                                        ALU.add).then_inc(hid_biased_cr, 1)

            def slot_step(j, s, turn, more=True):
                e_next = expert_of(j + 1) if more else None
                e = expert_of(j)
                if more:
                    dve.wait_ge(hid_turned_c1, j + 1)
                    bias_hidden(j + 1, 1 - s, e_next)
                dve.wait_ge(ys_made, j + 1)
                dve.wait_ge(d_ys_c1[s], 16 * turn + 16)
                nc.vector.tensor_tensor(ys_sb[:, s * D:(s + 1) * D], bank[6 + s][:, 0:D], b2_sb[:, ds(e * D, D)],
                                        ALU.add).then_inc(ys_set_cr, 1)

            bias_hidden(0, 0, expert_of(0))
            with dve.Fori(0, NS // 2 - 1) as i:
                slot_step(2 * i, 0, i)
                slot_step(2 * i + 1, 1, i)
            slot_step(NS - 2, 0, NS // 2 - 1)
            slot_step(NS - 1, 1, NS // 2 - 1, False)

            for n in range(2):
                dve.wait_ge(e_made, n + 1)
                link(nc.vector.tensor_tensor(Y[0], Y[0], Y[n + 1], ALU.add))
                nc.vector.tensor_tensor(Y[0], Y[0], bank[5 + 2 * n][:, :], ALU.add).then_inc(e_kept, 1)
                dve.wait_ge(e_kept, n + 1)

            def combine(t):
                n, s = real(t), t % 2
                dve.wait_ge(m1_set, t + 1)
                if t >= 2:
                    dve.wait_ge(moe_turned, t - 1)
                nc.vector.scalar_tensor_tensor(out=qn_sb[0:n, s * D:(s + 1) * D], in0=qk_sb[0:n, (NT + t) * D:(NT + t + 1) * D],
                                               scalar=wt_sb[0:n, 3 * NT + t:3 * NT + t + 1], in1=sq_sb[0:n, s * D:(s + 1) * D],
                                               op0=ALU.mult, op1=ALU.add).then_inc(moe_set, 1)

            def rotated(t):
                n, s = real(t), t % 2
                dve.wait_ge(rot_made, t + 1)
                mo = v_sb[0:n, t * D:(t + 1) * D]
                nc.vector.tensor_tensor(mo, bank[2 + s][0:n, 0:D], qn_sb[0:n, s * D:(s + 1) * D], ALU.add).then_inc(rot_kept, 1)
                dve.wait_ge(rot_kept, t + 1)
                nc.vector.tensor_tensor_reduce(att_sb[0:n, s * D:(s + 1) * D], mo, row_sb[0:n, R_GW + D:R_GW + 2 * D], 1.0,
                                               z_sb[0:n, t:t + 1], ALU.mult, ALU.add, z_sb[0:n, NT + t:NT + t + 1]).then_inc(z_set, 1)
                dve.wait_ge(z_set, t + 1)
                nc.vector.tensor_scalar(z_sb[0:n, NT + t:NT + t + 1], z_sb[0:n, NT + t:NT + t + 1], -87.0, None,
                                        ALU.max).then_inc(z_bounded, 1)

            def result(t):
                n = real(t)
                mo, o = v_sb[0:n, t * D:(t + 1) * D], h1_sb[0:n, t * D:(t + 1) * D]
                g = z_sb[0:n, 3 * NT + t:3 * NT + t + 1]
                nc.vector.tensor_tensor(mo, mo, o, ALU.subtract).then_inc(diff_set, 1)
                dve.wait_ge(gexp_set, t + 1)
                link(nc.vector.tensor_scalar(g, z_sb[0:n, 2 * NT + t:2 * NT + t + 1], 1.0, None, ALU.add))
                link(nc.vector.reciprocal(g, g))
                dve.wait_ge(diff_set, t + 1)
                nc.vector.scalar_tensor_tensor(out=o, in0=mo, scalar=g, in1=hb_sb[0:n, t * D:(t + 1) * D],
                                               op0=ALU.mult, op1=ALU.add).then_inc(out_set, 1)

            dve.wait_ge(abelw_set, 1)
            for k in range(NT + 2):
                if k < NT:
                    combine(k)
                if 1 <= k <= NT:
                    rotated(k - 1)
                if k >= 2:
                    result(k - 2)

        @block.tensor
        def _(pe):
            pe.sem_inc(hid_turned_c1, 1)

            def embed(t, slot, turn):
                pe.wait_ge(d_patch[slot], 16 * (turn + 1))
                pe.wait_ge(h_added_cr, t + 1)
                for k in range(FK):
                    if isinstance(t, int) and t == 0:
                        pe.wait_ge(d_tok[k], 16)
                    last = nc.tensor.matmul(bank[2 + slot % 2][0:T, 0:D], patch_sb[:, (slot * FK + k) * T:(slot * FK + k + 1) * T],
                                            wtok_sb[:, k * D:(k + 1) * D], start=(k == 0), stop=(k == FK - 1))
                last.then_inc(embedded, 1)

            for n in range(3):
                embed(n, n, 0)
            with pe.Fori(0, 2) as i:
                embed(4 * i + 3, 3, i)
                for n in range(3):
                    embed(4 * i + 4 + n, n, i + 1)

            pe.wait_ge(d_con, 48)

            def turn_two(dst, src):
                for c in range(2):
                    last = nc.tensor.transpose(dst[:, c * T:(c + 1) * T], src[:, c * 128:(c + 1) * 128], identT)
                return last

            def turn_x(t, s):
                pe.wait_ge(xh_set, t + 1)
                pe.wait_ge(xT_set_cr, t + 1)
                turn_two(bank[s], stage_sb[0:T, s * D:(s + 1) * D]).then_inc(xh_turned, 1)

            def qkv_step(t, s, more=True):
                if more:
                    turn_x(t + 1, 1 - s)
                pe.wait_ge(xT_set_cr, t + 3)
                pe.wait_ge(qk_squared_cr, t + 1)
                for k in range(2):
                    last = nc.tensor.matmul(bank[4 + s][0:T, :], xT_sb[:, (2 * s + k) * T:(2 * s + k + 1) * T],
                                            wqkv_sb[:, k * 3 * D:k * 3 * D + 2 * D], start=(k == 0), stop=(k == 1))
                last.then_inc(qk_made, 1)
                pe.wait_ge(v_kept_cr, t + 1)
                for k in range(2):
                    last = nc.tensor.matmul(bank[2 + s][0:T, 0:D], xT_sb[:, (2 * s + k) * T:(2 * s + k + 1) * T],
                                            wqkv_sb[:, k * 3 * D + 2 * D:(k + 1) * 3 * D], start=(k == 0), stop=(k == 1))
                last.then_inc(v_made, 1)

            pe.wait_ge(w_centred, 2)
            turn_x(0, 0)
            pairs(pe, qkv_step, NT - 1)
            qkv_step(NT - 1, 0, False)

            pe.wait_ge(consts_set, 2)
            pe.wait_ge(d_w, 16)

            def turn_qk(t, s, u, b, quarter):
                if quarter == 0:
                    pe.wait_ge(low_set, t + 1)
                if quarter == 2:
                    pe.wait_ge(low_k_set, t + 1)
                pe.wait_ge(evac_cr, u + 1)
                for n in range(4):
                    at = s * 8 * D + (4 * quarter + n) * 8 * HD
                    last = nc.tensor.transpose(bank[b][:, n * T:(n + 1) * T].bitcast(f32r), parts_sb[0:T, at:at + 8 * HD], ident_r[0:T, :])
                last.then_inc(turned, 1)

            mask4 = maskb_sb[0:T, :].unsqueeze(1).broadcast_to([T, 4, T])

            def scores(t, s, hf):
                pe.wait_ge(shifted_cr, 2 * t + hf + 1)
                for b in (4 + 2 * hf, 5 + 2 * hf):
                    nc.tensor.matmul(bank[b][0:T, 0:4 * T], idb_sb[0:T, :], mask4, start=True, stop=False, skip_group_check=True)
                for n in range(4 * hf, 4 * hf + 4):
                    q0, k0 = (24 * s + n) * T, (24 * s + 8 + 2 * n) * T
                    last = nc.tensor.matmul(bank[4 + n // 2][0:T, (n % 2) * 2 * T:(n % 2 + 1) * 2 * T], qkT_sb[:, q0:q0 + T],
                                            qkT_sb[:, k0:k0 + 2 * T], start=False, stop=True, skip_group_check=True)
                last.then_inc(scored, 1)

            def turn_probs(t, s, g, u, b):
                pe.wait_ge(probs_set, 2 * t + g // 2 + 1)
                pe.wait_ge(evac_cr, u + 1)
                for n in range(4):
                    h0 = (s * NH + 4 * g + n) * T
                    last = nc.tensor.transpose(bank[b][0:T, n * T:(n + 1) * T], p_sb[0:T, h0:h0 + T], identT)
                last.then_inc(turned, 1)

            def values(t, s, g, u, b):
                pe.wait_ge(evac_cr, u + 3)
                if g == 0:
                    pe.wait_ge(att_set_c1, t + 1)
                    pe.wait_ge(v_staged, t + 1)
                for n in range(4):
                    h = 4 * g + n
                    v0 = (s * NH + h) * VW
                    last = nc.tensor.matmul(bank[2][0:T, h * VW:(h + 1) * VW], pT_sb[0:T, ((g % 2) * 4 + n) * T:((g % 2) * 4 + n + 1) * T],
                                            keep_v_sb[0:T, v0:v0 + VW], start=True, stop=True, skip_group_check=True)
                last.then_inc(pv_made, 1)

            def turn_att(t, s, u, b):
                pe.wait_ge(att_set_c1, t + 2)
                pe.wait_ge(evac_cr, u + 1)
                turn_two(bank[b], att_sb[0:T, s * D:(s + 1) * D]).then_inc(turned, 1)

            def output(t, u, b):
                pe.wait_ge(evac_cr, u + 3)
                pe.wait_ge(h1_added_c1, t + 1)
                for k in range(2):
                    last = nc.tensor.matmul(bank[3][0:T, 0:D], attT_sb[:, k * T:(k + 1) * T], wo_sb[:, k * D:(k + 1) * D],
                                            start=(k == 0), stop=(k == 1))
                last.then_inc(wo_made, 1)

            def attn_step(t, s):
                u = uses(t, s)
                for hf in range(2):
                    if QK[2 * hf] in u:
                        turn_qk(t + 2, s, *u[QK[2 * hf]], 2 * hf)
                        turn_qk(t + 2, s, *u[QK[2 * hf + 1]], 2 * hf + 1)
                    if not last_tile(t):
                        pe.wait_ge(evac_cr, 8 + 2 if isinstance(t, int) and t == 0 else first_use(t) - 2)
                        scores(t + 1, 1 - s, hf)
                turn_probs(t, s, 0, *u["P0"])
                turn_probs(t, s, 1, *u["P1"])
                if "A" in u:
                    turn_att(t - 1, 1 - s, *u["A"])
                values(t, s, 0, *u["P0"])
                turn_probs(t, s, 2, *u["P2"])
                values(t, s, 1, *u["P1"])
                if "A" in u:
                    output(t - 1, *u["A"])
                turn_probs(t, s, 3, *u["P3"])
                values(t, s, 2, *u["P2"])
                values(t, s, 3, *u["P3"])

            pe.wait_ge(idr_set, 1)
            for n in range(4):
                turn_qk(0, 0, n, n % 2, n)
            pe.wait_ge(evac_cr, 4 + 2)
            scores(0, 0, 0)
            scores(0, 0, 1)
            for n in range(4):
                turn_qk(1, 1, 4 + n, n % 2, n)
            attn_tiles(pe, attn_step)
            turn_att(NT - 1, 0, *LAST_USE)
            output(NT - 1, *LAST_USE)

            def turn_z(t, s):
                pe.wait_ge(zs_set, t + 1)
                pe.wait_ge(zT_set_cr, t + 1)
                turn_two(bank[s], stage_sb[0:T, s * D:(s + 1) * D]).then_inc(z_turned, 1)

            def pre_step(t, s, more=True):
                if more:
                    turn_z(t + 1, 1 - s)
                pe.wait_ge(zT_set_cr, t + 3)
                pe.wait_ge(pre_kept_cr, t + 1)
                for k in range(2):
                    last = nc.tensor.matmul(bank[2 + s][0:T, 0:PW], xT_sb[:, (2 * s + k) * T:(2 * s + k + 1) * T],
                                            wpre_sb[:, k * PW:(k + 1) * PW], start=(k == 0), stop=(k == 1))
                last.then_inc(pre_made, 1)

            pe.wait_ge(d_pre, 16)
            turn_z(0, 0)
            pairs(pe, pre_step, NT - 1)
            pre_step(NT - 1, 0, False)

            def rank():
                pe.wait_ge(onehot_set, 1)
                L = E * NT
                for b, k in ((0, K_LOW), (1, K_ONE)):
                    last = nc.tensor.matmul(bank[b][0:T, 0:L], con_sb[0:T, k:k + T], rt_sb[0:T, 2 * L:3 * L], start=True, stop=True)
                last.then_inc(ranked, 1)

            def product(dst, xT, y):
                for m in range(2):
                    for k in range(2):
                        last = nc.tensor.matmul(dst[:, m * D:(m + 1) * D], xT[:, k * D + m * 128:k * D + (m + 1) * 128],
                                                y[:, k * D:(k + 1) * D], start=(k == 0), stop=(k == 1))
                return last

            def turn_square(dst, x):
                for m in range(2):
                    for k in range(2):
                        last = nc.tensor.transpose(dst[:, k * D + m * 128:k * D + (m + 1) * 128],
                                                   x[:, m * D + k * 128:m * D + (k + 1) * 128], ident)
                return last

            pe.wait_ge(n_scaled, 2)
            for n in range(G):
                product(bank[5 + n], AT[n], A[n]).then_inc(x_made, 1)
                if n == 1:
                    rank()
            pe.wait_ge(pre_kept_cr, NT + 2)
            for n in range(G):
                pe.wait_ge(x_kept, n + 1)
                product(bank[2 + n], AT[n], A2[n]).then_inc(x_made, 1)
            for n in range(G):
                pe.wait_ge(x_kept, G + n + 1)
                product(bank[5 + n], AT[n], A3[n]).then_inc(x_made, 1)
            pe.wait_ge(slots_set, 2)
            for n in range(G):
                pe.wait_ge(x_kept, 2 * G + n + 1)
                if n == 2:
                    pe.wait_ge(x_evac, 1)
                turn_square(bank[n % 2], A4[n]).then_inc(x_turned, 1)
            for m in range(2):
                for n in range(G):
                    pe.wait_ge(x_evac, n + 1)
                    pe.wait_ge(poly_set, G * m + n + 1)
                    product(bank[(2, 5)[m] + n], A4T[n], poly[n]).then_inc(p_made, 1)
            pe.wait_ge(y_set, G)
            squarings = pe.value_load(nrmi_sb[0:1, 2:3], min_val=SQUARINGS, max_val=20)
            with pe.Fori(0, squarings) as j:
                for n in range(G):
                    pe.wait_ge(s_kept_cr, 3 * j + n + 1)
                    turn_square(bank[n], Y[n]).then_inc(s_turned, 1)
                for n in range(G):
                    pe.wait_ge(s_evac, 3 * j + n + 1)
                    product(bank[5 + n], YT[n], Y[n]).then_inc(s_made, 1)

            pe.wait_ge(d_exp, 32)
            pe.wait_ge(experts_set, 1)
            pe.wait_ge(s_kept_cr, 3 * squarings + G)

            def turn_xs(j, s, turn):
                pe.wait_ge(d_xs[s], 16 * (turn + 1))
                pe.wait_ge(xsT_set, j)
                for c in range(2):
                    last = nc.tensor.transpose(bank[1][:, c * 128:(c + 1) * 128], xs_sb[:, s * D + c * 128:s * D + (c + 1) * 128], ident)
                last.then_inc(xs_turned, 1)

            def expert_of(j):
                return pe.value_load(ei_sb[0:1, ds(j, 1)], min_val=0, max_val=E - 1)

            def hidden(j, s, e):
                pe.wait_ge(xsT_set, j + 1)
                pe.wait_ge(hid_biased_cr, j + 1)
                for k in range(2):
                    last = nc.tensor.matmul(bank[4 + s][:, :], xsT_sb[:, (2 * s + k) * 128:(2 * s + k + 1) * 128],
                                            w1_sb[:, ds(e * 2 * HID + k * HID, HID)], start=(k == 0), stop=(k == 1))
                last.then_inc(hid_made, 1)

            def slot_step(j, s, turn, e, e_next, ahead=2):
                pe.wait_ge(gelu_set, j + 1)
                pe.wait_ge(hidT_set_c1, j + 1)
                for k in range(4):
                    last = nc.tensor.transpose(bank[0][:, k * 128:(k + 1) * 128], hid_sb[:, s * HID + k * 128:s * HID + (k + 1) * 128], ident)
                last.then_inc(hid_turned_c1, 1)
                if ahead == 2:
                    turn_xs(j + 2, s, turn + 1)
                if ahead >= 1:
                    hidden(j + 1, 1 - s, e_next)
                pe.wait_ge(hidT_set_c1, j + 2)
                pe.wait_ge(ys_set_cr, j + 1)
                for k in range(4):
                    last = nc.tensor.matmul(bank[6 + s][:, 0:D], hidT_sb[:, k * 128:(k + 1) * 128],
                                            w2_sb[:, ds(e * 4 * D + k * D, D)], start=(k == 0), stop=(k == 3))
                last.then_inc(ys_made, 1)

            turn_xs(0, 0, 0)
            hidden(0, 0, expert_of(0))
            turn_xs(1, 1, 0)
            with pe.Fori(0, NS // 2 - 1) as i:
                e = [expert_of(2 * i + n) for n in range(3)]
                slot_step(2 * i, 0, i, e[0], e[1])
                slot_step(2 * i + 1, 1, i, e[1], e[2])
            e = [expert_of(NS - 2 + n) for n in range(2)]
            slot_step(NS - 2, 0, None, e[0], e[1], 1)
            slot_step(NS - 1, 1, None, e[1], None, 0)

            pe.wait_ge(hid_biased_cr, NS + 2)
            pe.wait_ge(ys_set_cr, NS + 2)
            for n in range(2):
                if n:
                    pe.wait_ge(e_kept, n)
                turn_square(bank[4 + 2 * n], Y[0]).then_inc(e_turned, 1)
                pe.wait_ge(e_evac, n + 1)
                product(bank[5 + 2 * n], YT[n], Y[n + 1]).then_inc(e_made, 1)
            pe.wait_ge(e_kept, 2)

            def turn_moe(t):
                n, s = (T if t < NT - 1 else TLAST), t % 2
                pe.wait_ge(moe_set, t + 1)
                if t >= 2:
                    pe.wait_ge(moeT_set, t - 1)
                for c in range(2):
                    last = nc.tensor.transpose(bank[s][:, c * T:c * T + n], qn_sb[0:n, s * D + c * 128:s * D + (c + 1) * 128], con_sb[0:n, K_ID:K_ID + n])
                last.then_inc(moe_turned, 1)

            def rotate(t):
                n, s = (T if t < NT - 1 else TLAST), t % 2
                pe.wait_ge(moeT_set, t + 1)
                if t >= 2:
                    pe.wait_ge(rot_kept, t - 1)
                for k in range(2):
                    last = nc.tensor.matmul(bank[2 + s][0:n, 0:D], xT_sb[:, (2 * s + k) * T:(2 * s + k) * T + n],
                                            y_sb[:, k * D:(k + 1) * D], start=(k == 0), stop=(k == 1))
                last.then_inc(rot_made, 1)

            turn_moe(0)
            for t in range(1, NT):
                turn_moe(t)
                rotate(t - 1)
            rotate(NT - 1)


def _rows_to_partitions(a):
    a = np.asarray(a)
    k = a.shape[-2] // 128
    a = a.reshape(a.shape[:-2] + (k, 128, a.shape[-1]))
    return np.ascontiguousarray(np.moveaxis(a, -2, 0)).reshape(128, -1)


def _constants():
    con = np.zeros((128, NCONST), np.float32)
    p = np.arange(128)
    con[:, K_ID:K_ID + 128] = np.eye(128)
    q, m = np.meshgrid(np.arange(T), np.arange(T), indexing="ij")
    con[:T, K_MASK:K_MASK + T] = np.where((q // SEQ == m // SEQ) & (m <= q), 0.0, NEG)
    con[:, K_LOW:K_LOW + 128] = p[:, None] < p[None, :]
    con[:, K_ONE:K_ONE + 128] = 1.0
    con[:, K_IOTA:K_IOTA + 32] = np.arange(32)
    con[TLAST:, K_INV + NT - 1] = 100.0
    con[:, K_SEG:K_SEG + E * NT] = (np.arange(E * NT) % NT != 0)
    return con


def kernel(x, cls_tok, L0_tok_w, L0_tok_b, L0_tok_cls_token, L0_tok_pos, L0_attn_mask, L0_attn_Wq, L0_attn_Wk, L0_attn_Wv,
           L0_attn_gq, L0_attn_bq, L0_attn_gk, L0_attn_bk, L0_attn_Wo, L0_attn_bo, L0_ffn_ln_gamma, L0_ffn_ln_beta,
           L0_ffn_abel_w, L0_ffn_abel_b, L0_ffn_moe_gate_w, L0_ffn_moe_gate_b, L0_ffn_ew1, L0_ffn_eb1, L0_ffn_ew2,
           L0_ffn_eb2, L0_ffn_gens, L0_ffn_gc_w, L0_ffn_gc_b):
    import concourse.bacc as bacc
    from concourse.bass_utils import run_bass_kernel_spmd

    f32 = np.float32
    P = 16
    x = np.asarray(x)
    C, W = x.shape[1], x.shape[2] // P
    patches = x.reshape(B, C, W, P, W, P).transpose(0, 2, 4, 1, 3, 5).reshape(B, W * W, C * P * P)
    tok = np.zeros((NT * IPT, SEQ, C * P * P), f32)
    tok[:B, 2:] = patches
    tok = tok.reshape(NT, T, FK, 128).transpose(0, 3, 2, 1).reshape(NT, 128, FK * T)

    cols = np.zeros((128, NCOL), f32)
    cols[:, C_GAM:C_GAM + 2] = np.asarray(L0_ffn_ln_gamma).reshape(2, 128).T
    cols[:, C_BET:C_BET + 2] = np.asarray(L0_ffn_ln_beta).reshape(2, 128).T

    rows = np.zeros((128, NROW), f32)
    for n in range(IPT):
        r = n * SEQ
        rows[r, R_BASE:R_BASE + D] = np.asarray(cls_tok).reshape(D)
        rows[r + 1, R_BASE:R_BASE + D] = L0_tok_cls_token
        rows[r + 2:r + SEQ, R_BASE:R_BASE + D] = L0_tok_b
        rows[r + 1:r + SEQ, R_POS:R_POS + D] = L0_tok_pos
    rows[:, R_BO:R_BO + D] = L0_attn_bo
    rows[:, R_PRE:R_PRE + D] = L0_ffn_abel_b
    rows[:, R_PRE + D:R_PRE + PW] = L0_ffn_moe_gate_b
    rows[:, R_GW:R_GW + 2 * D] = np.asarray(L0_ffn_gc_w).reshape(2 * D)
    rows[:, R_GCB] = np.asarray(L0_ffn_gc_b)
    rows[:, R_QK:R_QK + 4 * HD] = np.concatenate([L0_attn_gq, L0_attn_gk, L0_attn_bq, L0_attn_bk])

    gens = np.asarray(L0_ffn_gens)
    arrays = {
        "patches": tok,
        "w_tok": _rows_to_partitions(np.asarray(L0_tok_w).T),
        "w_qkv": _rows_to_partitions(np.concatenate([L0_attn_Wq, L0_attn_Wk, L0_attn_Wv]).T),
        "w_o": _rows_to_partitions(np.asarray(L0_attn_Wo).T),
        "w_pre": _rows_to_partitions(np.concatenate([L0_ffn_abel_w, L0_ffn_moe_gate_w], axis=1)),
        "w1": _rows_to_partitions(L0_ffn_ew1),
        "w2": _rows_to_partitions(L0_ffn_ew2),
        "b1": np.asarray(L0_ffn_eb1).reshape(1, E * HID),
        "b2": np.asarray(L0_ffn_eb2).reshape(1, E * D),
        "gens": _rows_to_partitions(gens),
        "gens_t": _rows_to_partitions(gens.transpose(0, 2, 1)),
        "cols": cols, "rows": rows, "consts": _constants(),
    }
    nc = bacc.Bacc("TRN2", target_bir_lowering=False, num_devices=1)
    arrays = {f"in_{k}": np.ascontiguousarray(v) for k, v in arrays.items()}
    args = [nc.dram_tensor(k, v.shape, mybir.dt.from_np(v.dtype), kind="ExternalInput").ap() for k, v in arrays.items()]
    out = nc.dram_tensor("out_rows", (B * SEQ, D), mybir.dt.float32, kind="ExternalOutput").ap()
    vit_kernel(nc, *args, out)
    r = run_bass_kernel_spmd(nc, [arrays], core_ids=[0])
    return r.results[0]["out_rows"].reshape(B, SEQ, D)
```
